# Optimizing a Trainium2 kernel written in Bass

```python
import numpy as np
import jax
import jax.numpy as jnp

def _softmax(x, axis=-1):
    return jax.nn.softmax(x, axis=axis)

def _gelu(x):
    return jax.nn.gelu(x, approximate=True)

def _silu(x):
    return jax.nn.silu(x)

def _sigmoid(x):
    return jax.nn.sigmoid(x)

def _layernorm(x, axis=-1, eps=1e-05):
    m = jnp.mean(x, axis=axis, keepdims=True)
    v = jnp.var(x, axis=axis, keepdims=True)
    return (x - m) / jnp.sqrt(v + eps)

def _scatter_add(tgt, idx, src, axis=0):
    return tgt.at[idx].add(src)

def _segment_sum(src, seg, n):
    return jax.ops.segment_sum(src, seg, n)
kernel_name = 'mk_xattn_seq_d2_seqx_r4_68b0c5'

def setup_inputs(seed: int=0):
    np.random.seed(seed)
    _w = jnp.asarray

    def _rec_inputs():
        import jax
        import jax.numpy as jnp
        _rk = jax.random.key(seed)
        x = -0.000125 + 0.9999 * jax.random.normal(jax.random.fold_in(_rk, 1), (32, 128, 1024), jnp.float32)
        _lenS = 128 - jax.random.randint(jax.random.fold_in(_rk, 7), (32,), 0, max(1, 128 // 4) + 1, jnp.int32)
        _lenS2 = 128 - jax.random.randint(jax.random.fold_in(_rk, 8), (32,), 0, max(1, 128 // 4) + 1, jnp.int32)
        _ctx_4096P = jax.random.normal(jax.random.fold_in(_rk, 11), (32, 16, 1024), jnp.float32)
        _ctx_4096c = jax.random.dirichlet(jax.random.fold_in(_rk, 511), 0.3 * jnp.ones((16,), jnp.float32), (32, 128))
        _ctx_4096t = jnp.einsum('bsk,bkd->bsd', _ctx_4096c, _ctx_4096P)
        _ctx_4096t = _ctx_4096t * jax.lax.rsqrt(jnp.mean(jnp.square(_ctx_4096t)) + 1e-12) * 0.953939
        ctx_4096 = -1.52775e-05 + 0.999936 * (_ctx_4096t + 0.3 * jax.random.normal(jax.random.fold_in(_rk, 611), (32, 128, 1024), jnp.float32))
        return (x, ctx_4096)
    x, ctx_4096 = _rec_inputs()

    def _L0_xattn_setup():
        import jax, jax.numpy as jnp
        import numpy as np
        B, C, N, H = (16, 128, 1024, 8)
        key = jax.random.key(seed)
        ks = jax.random.split(key, 10)
        s = 0.02
        return {'rgb_emb': jax.random.normal(ks[0], (B, C, N), jnp.float32), 'geo_emb': jax.random.normal(ks[1], (B, C, N), jnp.float32), 'wq_rgb': jax.random.normal(ks[2], (C, C), jnp.float32) * s, 'wk_rgb': jax.random.normal(ks[3], (C, C), jnp.float32) * s, 'wv_rgb': jax.random.normal(ks[4], (C, C), jnp.float32) * s, 'wq_point': jax.random.normal(ks[5], (C, C), jnp.float32) * s, 'wk_point': jax.random.normal(ks[6], (C, C), jnp.float32) * s, 'wv_point': jax.random.normal(ks[7], (C, C), jnp.float32) * s, 'proj_r2p': jax.random.normal(ks[8], (C, C), jnp.float32) * s, 'proj_p2r': jax.random.normal(ks[9], (C, C), jnp.float32) * s}
    _L0_xattn_all = _L0_xattn_setup()
    _L0_xattn_in = {k: v for k, v in _L0_xattn_all.items() if k in ('wq_rgb', 'wk_rgb', 'wv_rgb', 'wq_point', 'wk_point', 'wv_point', 'proj_r2p', 'proj_p2r')}
    del _L0_xattn_all

    def _L1_xattn_setup():
        import jax, jax.numpy as jnp
        import numpy as np
        NUM_HEADS = 8
        EPS = 1e-05

        def _conv1x1(W, b, t):
            return jnp.einsum('oc,bcl->bol', W, t) + b[None, :, None]
        key = jax.random.key(seed)
        ks = jax.random.split(key, 12)
        B, C, E, L = (16, 128, 128, 1024)
        s = lambda k, shape, sc=1.0: jax.random.normal(k, shape, dtype=jnp.float32) * sc
        return {'x': s(ks[0], (B, E, L)), 'y': s(ks[1], (B, C, L)), 'Wq': s(ks[2], (E, C), 0.02), 'bq': jnp.zeros((E,), jnp.float32), 'Wk': s(ks[3], (E, C), 0.02), 'bk': jnp.zeros((E,), jnp.float32), 'Wv': s(ks[4], (E, E), 0.02), 'bv': jnp.zeros((E,), jnp.float32), 'Wo': s(ks[5], (E, E), 0.02), 'bo': jnp.zeros((E,), jnp.float32), 'gn_w': jnp.ones((E,), jnp.float32), 'gn_b': jnp.zeros((E,), jnp.float32)}
    _L1_xattn_all = _L1_xattn_setup()
    _L1_xattn_in = {k: v for k, v in _L1_xattn_all.items() if k in ('Wq', 'bq', 'Wk', 'bk', 'Wv', 'bv', 'Wo', 'bo', 'gn_w', 'gn_b')}
    del _L1_xattn_all
    return {'x': x, 'ctx_4096': ctx_4096, 'L0_xattn_wq_rgb': _L0_xattn_in['wq_rgb'], 'L0_xattn_wk_rgb': _L0_xattn_in['wk_rgb'], 'L0_xattn_wv_rgb': _L0_xattn_in['wv_rgb'], 'L0_xattn_wq_point': _L0_xattn_in['wq_point'], 'L0_xattn_wk_point': _L0_xattn_in['wk_point'], 'L0_xattn_wv_point': _L0_xattn_in['wv_point'], 'L0_xattn_proj_r2p': _L0_xattn_in['proj_r2p'], 'L0_xattn_proj_p2r': _L0_xattn_in['proj_p2r'], 'L1_xattn_Wq': _L1_xattn_in['Wq'], 'L1_xattn_bq': _L1_xattn_in['bq'], 'L1_xattn_Wk': _L1_xattn_in['Wk'], 'L1_xattn_bk': _L1_xattn_in['bk'], 'L1_xattn_Wv': _L1_xattn_in['Wv'], 'L1_xattn_bv': _L1_xattn_in['bv'], 'L1_xattn_Wo': _L1_xattn_in['Wo'], 'L1_xattn_bo': _L1_xattn_in['bo'], 'L1_xattn_gn_w': _L1_xattn_in['gn_w'], 'L1_xattn_gn_b': _L1_xattn_in['gn_b']}

def reference(x, ctx_4096, L0_xattn_wq_rgb, L0_xattn_wk_rgb, L0_xattn_wv_rgb, L0_xattn_wq_point, L0_xattn_wk_point, L0_xattn_wv_point, L0_xattn_proj_r2p, L0_xattn_proj_p2r, L1_xattn_Wq, L1_xattn_bq, L1_xattn_Wk, L1_xattn_bk, L1_xattn_Wv, L1_xattn_bv, L1_xattn_Wo, L1_xattn_bo, L1_xattn_gn_w, L1_xattn_gn_b):
    import jax
    import jax.numpy as jnp

    def _L0_xattn_ref(rgb_emb, geo_emb, wq_rgb, wk_rgb, wv_rgb, wq_point, wk_point, wv_point, proj_r2p, proj_p2r):
        import jax, jax.numpy as jnp
        import numpy as np
        B, C, N, H = (16, 128, 1024, 8)
        rgb = jnp.transpose(rgb_emb, (0, 2, 1))
        geo = jnp.transpose(geo_emb, (0, 2, 1))
        b, n, c = rgb.shape
        d = c // H
        scale = d ** (-0.5)

        def heads(x, w):
            return (x @ w.T).reshape(b, n, H, d).transpose(0, 2, 1, 3)

        def xca(q, k, v):
            attn = jax.nn.softmax(jnp.einsum('bhni,bhnj->bhij', q, k) * scale, axis=-1)
            out = jnp.einsum('bhnd,bhde->bhne', v, attn)
            return out.transpose(0, 2, 1, 3).reshape(b, n, c)
        res_p2r = xca(heads(rgb, wq_rgb), heads(geo, wk_point), heads(geo, wv_point)) @ proj_p2r.T
        res_r2p = xca(heads(geo, wq_point), heads(rgb, wk_rgb), heads(rgb, wv_rgb)) @ proj_r2p.T
        rgb_att = jnp.transpose(rgb + res_p2r, (0, 2, 1))
        geo_att = jnp.transpose(geo + res_r2p, (0, 2, 1))
        return rgb_att + geo_att

    def _L1_xattn_ref(x, y, Wq, bq, Wk, bk, Wv, bv, Wo, bo, gn_w, gn_b):
        import jax, jax.numpy as jnp
        import numpy as np
        NUM_HEADS = 8
        EPS = 1e-05

        def _conv1x1(W, b, t):
            return jnp.einsum('oc,bcl->bol', W, t) + b[None, :, None]
        B, E, Lx = x.shape
        H = NUM_HEADS
        Dh = E // H
        q = _conv1x1(Wq, bq, y).reshape(B, H, Dh, -1)
        k = _conv1x1(Wk, bk, y).reshape(B, H, Dh, -1)
        v = _conv1x1(Wv, bv, x).reshape(B, H, Dh, Lx)
        scores = jnp.einsum('bhdl,bhel->bhde', q, k) / jnp.sqrt(jnp.float32(E))
        attn = jax.nn.softmax(scores, axis=-1)
        out = jnp.einsum('bhde,bhel->bhdl', attn, v).reshape(B, E, Lx)
        o = _conv1x1(Wo, bo, out) + x
        mu = jnp.mean(o, axis=(1, 2), keepdims=True)
        var = jnp.var(o, axis=(1, 2), keepdims=True)
        o_hat = (o - mu) * jax.lax.rsqrt(var + EPS)
        return o_hat * gn_w[None, :, None] + gn_b[None, :, None]
    x = _L0_xattn_ref(x, ctx_4096, L0_xattn_wq_rgb, L0_xattn_wk_rgb, L0_xattn_wv_rgb, L0_xattn_wq_point, L0_xattn_wk_point, L0_xattn_wv_point, L0_xattn_proj_r2p, L0_xattn_proj_p2r)
    x = _L1_xattn_ref(x, ctx_4096, L1_xattn_Wq, L1_xattn_bq, L1_xattn_Wk, L1_xattn_bk, L1_xattn_Wv, L1_xattn_bv, L1_xattn_Wo, L1_xattn_bo, L1_xattn_gn_w, L1_xattn_gn_b)
    return x

_drawn_inputs = setup_inputs


def setup_inputs(seed=0):
    import zlib

    import numpy as np

    out = dict(_drawn_inputs(seed))
    spreads = {'L1_xattn_bq': (0.0, 0.622),
     'L1_xattn_bk': (0.0, 0.62),
     'L1_xattn_bv': (0.0, 0.8),
     'L1_xattn_bo': (0.0, 0.1),
     'L1_xattn_gn_w': (1.0, 0.2),
     'L1_xattn_gn_b': (0.0, 0.1)}
    factors = {'L0_xattn_wq_rgb': 8.0,
     'L0_xattn_wk_rgb': 8.0,
     'L0_xattn_wv_rgb': 5.76,
     'L0_xattn_wq_point': 8.0,
     'L0_xattn_wk_point': 8.0,
     'L0_xattn_wv_point': 6.109,
     'L0_xattn_proj_r2p': 5.615,
     'L0_xattn_proj_p2r': 5.841,
     'L1_xattn_Wq': 3.15,
     'L1_xattn_Wk': 2.889}
    for name, (base, spread) in spreads.items():
        noise = np.random.default_rng([zlib.crc32(name.encode()), seed]).standard_normal(out[name].shape)
        drawn = base * np.exp(spread * noise) if base else spread * noise
        out[name] = jnp.asarray(drawn.astype(out[name].dtype))
    for name, factor in factors.items():
        out[name] = (out[name] * factor).astype(out[name].dtype)
    return out
```

```python
import concourse.bass as bass
from concourse import mybir
from concourse.alu_op_type import AluOpType as ALU
from contextlib import ExitStack

B, C, N, H = 32, 128, 1024, 8
EPS = 1e-5
PAIRS = B // 2
CH = N // C
QT = 4
HALF = N // 2
W32 = 32
NEG = -1e30

WNAMES = ["kpT", "qpT", "kT", "qrT", "krT", "qT", "vp", "vr", "oT", "ppT", "prT", "v", "bk_rows", "bq_rows"]
VNAMES = ["bk", "bo", "gn_w", "gn_b"]


def cross_attention_pair_kernel(nc, x, y, weights, vectors, bv_rows, consts, out):
    f32, f32r = mybir.dt.float32, mybir.dt.float32r
    ACT = mybir.ActivationFunctionType
    AX = mybir.AxisListType

    ctx = ExitStack()
    with ctx:
        def sb(name, shape, dt=f32):
            return ctx.enter_context(nc.sbuf_tensor(name, shape, dt))

        def pb(name, shape):
            return ctx.enter_context(nc.psum_tensor(name, shape, f32))

        def sem(name):
            return ctx.enter_context(nc.semaphore(name))

        wt = sb("wt", [C, len(WNAMES), C])
        vec = sb("vec", [C, len(VNAMES)])
        bvr = sb("bvr", [C, W32])
        cst = sb("cst", [C, 3 * C + 2 * W32 + 3])
        ident = cst[:, 0:C]
        same_head = cst[:, C:2 * C]
        mean_w = cst[:, 2 * C:3 * C]
        other_head = cst[:, 3 * C:3 * C + W32]
        diag32 = cst[:, 3 * C + W32:3 * C + 2 * W32]
        zero_eps = cst[:, 3 * C + 2 * W32:3 * C + 2 * W32 + 2]
        neg_half = cst[:, 3 * C + 2 * W32 + 2:3 * C + 2 * W32 + 3]

        def w(name):
            return wt[:, WNAMES.index(name), :]

        def col(name):
            k = VNAMES.index(name)
            return vec[:, k:k + 1]

        bq_head = sb("bq_head", [C, C])
        nbk32 = sb("nbk32", [C, W32])
        raw = [sb(f"raw{n}", [C, 2, N]) for n in range(4)]
        xy_hi = [sb(f"xy_hi{n}", [C, 2, N], f32r) for n in range(4)]
        xy_lo = [sb(f"xy_lo{n}", [C, 2, N], f32r) for n in range(4)]
        t_hi = [sb(f"t_hi{n}", [C, CH, 2 * C + 2], f32r) for n in range(2)]
        t_lo = [sb(f"t_lo{n}", [C, CH, 2 * C], f32r) for n in range(2)]
        gram = sb("gram", [C, 2, 2 * C + 2])
        u12 = sb("u12", [C, 2, 2, C])
        u3 = sb("u3", [C, 2, C])
        krow = sb("krow", [C, 2, W32])
        sc_m = sb("sc_m", [C, 6, W32])
        sc_d = sb("sc_d", [C, 6, W32])
        probs = sb("probs", [C, 6, W32])
        smax = sb("smax", [C, 6])
        ssum = sb("ssum", [C, 6])
        sinv = sb("sinv", [C, 6])
        attn = sb("attn", [C, 6, C])
        abv_m = sb("abv_m", [C, 2, W32])
        abv_s = sb("abv_s", [C, 2])
        abv = sb("abv", [C, 2])
        z = sb("z", [C, 3, 2, C])
        nmat = sb("nmat", [C, 3, 2, C])
        cshift = [sb(f"cshift{n}", [C, 2]) for n in range(2)]
        pq_hi = [sb(f"pq_hi{n}", [C, 2, 2, C], f32r) for n in range(2)]
        pq_lo = [sb(f"pq_lo{n}", [C, 2, 2, C], f32r) for n in range(2)]
        gate = sb("gate", [1, 4])
        hstat = sb("hstat", [C, 2, 6])
        pstat = sb("pstat", [C, 2])
        mom = sb("mom", [C, 2])
        gmom = sb("gmom", [C, 2])
        nvar = sb("nvar", [C, 1])
        var = sb("var", [C, 1])
        rstd = sb("rstd", [C, 1])
        cmu = sb("cmu", [C, 1])
        nscale = sb("nscale", [C, 1])
        nbias = sb("nbias", [C, 1])
        res = [sb(f"res{n}", [C, N]) for n in range(2)]

        tp = [pb(f"tp{n}", [C, 2, 2 * C]) for n in range(2)]
        gacc = pb("gacc", [C, HALF])
        mid0 = pb("mid0", [C, HALF])
        mid1 = pb("mid1", [C, HALF])
        stat = pb("stat", [C, HALF])
        oacc = [pb(f"oacc{n}", [C, HALF]) for n in range(2)]

        consts_in = sem("consts_in")
        loaded = [sem(f"loaded{n}") for n in range(4)]
        stored = [sem(f"stored{n}") for n in range(2)]
        prepared = sem("prepared")
        attn_zero = sem("attn_zero")
        ones_set = sem("ones_set")
        transposed = sem("transposed")
        thi_ready = sem("thi_ready")
        tlo_ready = sem("tlo_ready")
        gram_done = sem("gram_done")
        gram_ready = sem("gram_ready")
        u_done = sem("u_done")
        u12_ready = sem("u12_ready")
        u3_ready = sem("u3_ready")
        scores_done = sem("scores_done")
        masked = sem("masked")
        max_ready = sem("max_ready")
        shifted = sem("shifted")
        exp_ready = sem("exp_ready")
        sum_ready = sem("sum_ready")
        inv_ready = sem("inv_ready")
        attn_ready = sem("attn_ready")
        abv_step = sem("abv_step")
        abv_ready = sem("abv_ready")
        z_done = sem("z_done")
        z12_ready = sem("z12_ready")
        z3_ready = sem("z3_ready")
        m_done = sem("m_done")
        n_ready = sem("n_ready")
        pq_done = sem("pq_done")
        pqhi_ready = sem("pqhi_ready")
        pqlo_ready = sem("pqlo_ready")
        split_hi = sem("split_hi")
        split_lo = sem("split_lo")
        o_done = sem("o_done")
        hstat_ready = sem("hstat_ready")
        pstat_ready = sem("pstat_ready")
        mean_ready = sem("mean_ready")
        mom_ready = sem("mom_ready")
        stat_done = sem("stat_done")
        gmom_ready = sem("gmom_ready")
        nvar_ready = sem("nvar_ready")
        var_ready = sem("var_ready")
        rstd_ready = sem("rstd_ready")
        nscale_ready = sem("nscale_ready")
        norm_ready = sem("norm_ready")
        normed = sem("normed")

        def steps(eng, step):
            step(0, 0, True, False, False)
            step(0, 1, True, True, False)
            with eng.Fori(1, PAIRS // 2) as i:
                step(i, 0, True, True, True)
                step(i, 1, True, True, True)
            step(PAIRS // 2, 0, False, True, True)
            step(PAIRS // 2, 1, False, False, True)

        block = ctx.enter_context(nc.Block())

        @block.sync
        def _(sp):
            def load(h, u, b):
                n = 2 * u + b
                sp.dma_start(raw[n][:, 0, :], x[4 * h + n]).then_inc(loaded[n], 16)
                sp.dma_start(raw[n][:, 1, :], y[4 * h + n]).then_inc(loaded[n], 16)

            load(0, 0, 0)
            sp.dma_start(cst[:, :], consts).then_inc(consts_in, 16)
            sp.dma_start(wt[:, :, :], weights).then_inc(consts_in, 16)
            sp.dma_start(vec[:, :], vectors).then_inc(consts_in, 16)
            sp.dma_start(bvr[:, :], bv_rows).then_inc(consts_in, 16)
            load(0, 0, 1)
            load(0, 1, 0)
            load(0, 1, 1)

            def step(h, u, front, middle, back, refill=True):
                for b in range(2):
                    n = 4 * h + 2 * u + b
                    if back:
                        q = n - 4
                        sp.wait_ge(normed, 2 * q + 4)
                        sp.dma_start(out[q], res[b][:, :]).then_inc(stored[b], 16)
                    if front and refill:
                        sp.wait_ge(split_hi, 2 * n + 2)
                        sp.wait_ge(split_lo, 2 * n + 2)
                        sp.wait_ge(transposed, QT * (n + 1))
                        load(h + 1, u, b)

            step(0, 0, True, False, False)
            step(0, 1, True, True, False)
            with sp.Fori(1, PAIRS // 2 - 1) as i:
                step(i, 0, True, True, True)
                step(i, 1, True, True, True)
            last = PAIRS // 2 - 1
            step(last, 0, True, True, True, refill=False)
            step(last, 1, True, True, True, refill=False)
            step(last + 1, 0, False, True, True)
            step(last + 1, 1, False, False, True)
            for b in range(2):
                sp.wait_ge(stored[b], 16 * (B // 2 + 1))

        @block.tensor
        def _(pe):
            pe.wait_ge(consts_in, 64)
            pe.wait_ge(prepared, 5)
            pe.wait_ge(ones_set, 2)

            def transposes(h, u, j):
                b, k = divmod(j, QT)
                slot = 2 * u + b
                t = QT * (4 * h + slot) + k
                if k == 0:
                    pe.wait_ge(loaded[slot], 32 * (h + 1))
                if not (isinstance(t, int) and t < 2):
                    pe.wait_ge(tlo_ready, t - 1)
                for c in range(2):
                    for s in range(2):
                        src = raw[slot][:, s, (2 * k + c) * C:(2 * k + c + 1) * C]
                        mm = pe.transpose(tp[k % 2][:, c, s * C:(s + 1) * C], src, ident)
                mm.then_inc(transposed, 1)

            def gram_quarter(h, u, j):
                b, k = divmod(j, QT)
                n = 4 * h + 2 * u + b
                pe.wait_ge(tlo_ready, QT * n + k + 1)
                if k == 0 and not (isinstance(n, int) and n < 1):
                    pe.wait_ge(gram_ready, n)
                for c in range(2 * k, 2 * k + 2):
                    yhi, ylo = t_hi[b][:, c, C:2 * C], t_lo[b][:, c, C:2 * C]
                    pe.matmul(gacc[:, 0:2 * C + 2], yhi, t_hi[b][:, c, :], start=(c == 0), stop=False)
                    pe.matmul(gacc[:, 0:2 * C], yhi, t_lo[b][:, c, :], start=False, stop=False,
                              skip_group_check=True)
                    mm = pe.matmul(gacc[:, 0:2 * C + 2], ylo, t_hi[b][:, c, :], start=False,
                                   stop=(c == CH - 1))
                if k == QT - 1:
                    mm.then_inc(gram_done, 1)

            def out_half(h, u, b, half):
                slot = 2 * u + b
                n = 4 * h + slot
                if half == 0:
                    if b == 0:
                        pe.wait_ge(pqlo_ready, 2 * h + u + 1)
                    pe.wait_ge(split_hi, 2 * n + 2)
                    pe.wait_ge(split_lo, 2 * n + 2)
                pe.wait_ge(normed, 2 * n + 1 + half)
                cols = slice(half * HALF, (half + 1) * HALF)
                for s in range(2):
                    whi, wlo = pq_hi[u][:, b, s, :], pq_lo[u][:, b, s, :]
                    pe.matmul(oacc[half][:, :], whi, xy_hi[slot][:, s, cols], start=(s == 0), stop=False)
                    pe.matmul(oacc[half][:, :], whi, xy_lo[slot][:, s, cols], start=False, stop=False)
                    mm = pe.matmul(oacc[half][:, :], wlo, xy_hi[slot][:, s, cols], start=False, stop=(s == 1))
                mm.then_inc(o_done, 1)

            def group_moments(n):
                pe.wait_ge(mom_ready, n + 1)
                pe.matmul(stat[:, 0:2], mean_w, mom[:, :], start=True, stop=True).then_inc(stat_done, 1)

            def u_products(p):
                pe.wait_ge(gram_ready, 2 * p + 2)
                if not (isinstance(p, int) and p < 1):
                    pe.wait_ge(pqlo_ready, p)
                for a in range(2):
                    pe.matmul(mid0[:, a * 2 * C:(a + 1) * 2 * C], gram[:, a, 0:C], wt[:, 0:2, :],
                              start=True, stop=True)
                for a in range(2):
                    pe.matmul(mid1[:, a * C:(a + 1) * C], gram[:, a, C:2 * C], w("kT"), start=True, stop=True)
                pe.matmul(mid1[:, 2 * C:2 * C + 2], w("kT"), gram[:, :, 2 * C], start=True, stop=True)\
                    .then_inc(u_done, 1)

            def scores(p):
                pe.wait_ge(u12_ready, p + 1)
                pe.wait_ge(u3_ready, p + 1)
                for j in range(4):
                    q = slice(W32 * j, W32 * (j + 1))
                    s1 = mid0[q, 0:2 * W32]
                    pe.matmul(s1, w("qrT")[:, q], u12[:, :, 0, q], start=True, stop=True)
                for j in range(4):
                    q = slice(W32 * j, W32 * (j + 1))
                    s3 = mid0[q, 4 * W32:6 * W32]
                    pe.matmul(s3, w("qT")[:, q], u3[:, :, q], start=True, stop=False)
                for j in range(4):
                    q = slice(W32 * j, W32 * (j + 1))
                    s3 = mid0[q, 4 * W32:6 * W32]
                    pe.matmul(s3, bq_head[:, q], krow[:, :, :], start=False, stop=True)
                for a in range(2):
                    for j in range(4):
                        q = slice(W32 * j, W32 * (j + 1))
                        s2 = mid0[q, (2 + a) * W32:(3 + a) * W32]
                        mm = pe.matmul(s2, u12[:, a, 1, q], w("krT")[:, q], start=True, stop=True)
                mm.then_inc(scores_done, 1)

            def z_products(p):
                pe.wait_ge(attn_ready, p + 1)
                for i, name in enumerate(("vp", "vr", "oT")):
                    for a in range(2):
                        dst = mid1[:, (2 * i + a) * C:(2 * i + a + 1) * C] if i < 2 else mid0[:, a * C:(a + 1) * C]
                        mm = pe.matmul(dst, attn[:, 2 * i + a, :], w(name), start=True, stop=True)
                mm.then_inc(z_done, 1)

            def m_products(p):
                pe.wait_ge(z12_ready, p + 1)
                pe.wait_ge(z3_ready, p + 1)
                pe.matmul(mid1[:, 0:2 * C], w("ppT"), z[:, 0, :, :], start=True, stop=True)
                pe.matmul(mid1[:, 2 * C:4 * C], w("prT"), z[:, 1, :, :], start=True, stop=True)
                pe.matmul(mid0[:, 0:2 * C], w("v"), z[:, 2, :, :], start=True, stop=True)
                pe.wait_ge(abv_ready, p + 1)
                pe.matmul(mid0[:, 2 * C:2 * C + 2], w("oT"), abv[:, :], start=True, stop=True).then_inc(m_done, 1)

            def pq_products(p):
                pe.wait_ge(n_ready, p + 1)
                for a in range(2):
                    for s in range(2):
                        k = 2 * a + s
                        mm = pe.matmul(mid1[:, k * C:(k + 1) * C], nmat[:, 1 - s, a, :], nmat[:, 2, a, :],
                                       start=True, stop=True)
                mm.then_inc(pq_done, 1)

            def step(h, u, front, middle, back):
                p = 2 * h + u
                for j in range(2 * QT):
                    b, k = divmod(j, QT)
                    if front:
                        transposes(h, u, j)
                    if back and k < 2:
                        out_half(h - 1, u, b, k)
                    if middle:
                        if j == 0:
                            gram_quarter(*((h, 0) if u else (h - 1, 1)), 2 * QT - 1)
                        if j == 1:
                            u_products(p - 1)
                        if j == 3:
                            scores(p - 1)
                        if j == 5:
                            z_products(p - 1)
                        if j == 6:
                            m_products(p - 1)
                        if j == 7:
                            pq_products(p - 1)
                    if front and j > 0:
                        gram_quarter(h, u, j - 1)
                    if back and k == 2:
                        group_moments(4 * h + 2 * u + b - 4)

            steps(pe, step)

        @block.scalar
        def _(act):
            def high_part(h, u, j):
                b, k = divmod(j, QT)
                n = 4 * h + 2 * u + b
                act.wait_ge(transposed, QT * n + k + 1)
                if k == 0 and not (isinstance(n, int) and n < 2):
                    act.wait_ge(gram_done, n - 1)
                act.activation(t_hi[b][:, 2 * k:2 * k + 2, 0:2 * C], tp[k % 2][:, :, :], ACT.Copy)\
                    .then_inc(thi_ready, 1)

            def gram_out(h, u, b):
                n = 4 * h + 2 * u + b
                p = 2 * h + u
                act.wait_ge(gram_done, n + 1)
                if b == 0 and not (isinstance(p, int) and p < 1):
                    act.wait_ge(u_done, p)
                    act.wait_ge(u3_ready, p)
                act.activation(gram[:, b, :], gacc[:, 0:2 * C + 2], ACT.Copy).then_inc(gram_ready, 1)

            def split_high(h, u, b, s, back):
                slot = 2 * u + b
                n = 4 * h + slot
                act.wait_ge(loaded[slot], 32 * (h + 1))
                if s == 0 and back:
                    act.wait_ge(o_done, 2 * n - 6)
                act.activation(xy_hi[slot][:, s, :], raw[slot][:, s, :], ACT.Copy).then_inc(split_hi, 1)

            def normalise(h, u, b):
                n = 4 * h + 2 * u + b
                act.wait_ge(norm_ready, n + 1)
                act.wait_ge(stored[b], 16 * (2 * h + u + 1))
                for half in range(2):
                    act.activation(res[b][:, half * HALF:(half + 1) * HALF], oacc[half][:, :], ACT.Identity,
                                   bias=nbias[:, :], scale=nscale[:, :]).then_inc(normed, 1)

            def step(h, u, front, middle, back):
                p = 2 * h + u
                for j in range(2 * QT):
                    b, k = divmod(j, QT)
                    if front:
                        high_part(h, u, j)
                    if middle and j == 0:
                        gram_out(*((h, 0) if u else (h - 1, 1)), 1)
                    if middle and j == 1:
                        act.wait_ge(u_done, p)
                        act.activation(u12[:, :, :, :], mid0[:, :], ACT.Copy).then_inc(u12_ready, 1)
                    if front and k == 2:
                        split_high(h, u, b, 0, back)
                    if front and k == 3:
                        split_high(h, u, b, 1, back)
                    if middle and j == 3:
                        act.wait_ge(shifted, p)
                        act.activation(probs[:, :, :], sc_d[:, :, :], ACT.Exp).then_inc(exp_ready, 1)
                    if front and j == QT:
                        gram_out(h, u, 0)
                    if middle and j == 5:
                        act.wait_ge(z_done, p)
                        act.activation(z[:, 0:2, :, :], mid1[:, :], ACT.Copy).then_inc(z12_ready, 1)
                    if middle and j == 7:
                        act.wait_ge(pq_done, p)
                        act.activation(pq_hi[1 - u][:, :, :, :], mid1[:, :], ACT.Copy).then_inc(pqhi_ready, 1)
                    if back and k == 3:
                        normalise(h - 1, u, b)

            steps(act, step)

        @block.vector
        def _(dve):
            dve.memset(t_hi[0][:, :, 2 * C:].bitcast(f32), 1.0).then_inc(ones_set, 1)
            dve.memset(t_hi[1][:, :, 2 * C:].bitcast(f32), 1.0).then_inc(ones_set, 1)
            dve.memset(attn[:, :, :], 0.0).then_inc(attn_zero, 1)
            dve.memset(gate[:, 1:2], 0.0).then_inc(normed, 2)
            for b in range(2):
                dve.memset(gate[:, 2 + b:3 + b], 0.0).then_inc(stored[b], 16)
            dve.wait_ge(consts_in, 64)
            s0, s1 = float(C // H) ** -0.5, float(C) ** -0.5
            dve.tensor_scalar(w("qpT"), w("qpT"), s0, None, ALU.mult).then_inc(prepared, 1)
            dve.tensor_scalar(w("qrT"), w("qrT"), s0, None, ALU.mult).then_inc(prepared, 1)
            dve.tensor_scalar(w("qT"), w("qT"), s1, None, ALU.mult).then_inc(prepared, 1)
            dve.scalar_tensor_tensor(out=bq_head[:, :], in0=w("bq_rows"), scalar=s1, in1=same_head,
                                     op0=ALU.mult, op1=ALU.mult).then_inc(prepared, 1)
            dve.tensor_scalar(nbk32[:, :], diag32, col("bk"), float(N), ALU.mult, ALU.mult).then_inc(prepared, 1)
            dve.wait_ge(prepared, 5)
            dve.wait_ge(attn_zero, 1)

            def low_part(h, u, j):
                b, k = divmod(j, QT)
                t = QT * (4 * h + 2 * u + b) + k
                dve.wait_ge(thi_ready, t + 1)
                dve.tensor_tensor(t_lo[b][:, 2 * k:2 * k + 2, :], tp[k % 2][:, :, :],
                                  t_hi[b][:, 2 * k:2 * k + 2, 0:2 * C].bitcast(f32), ALU.subtract)\
                    .then_inc(tlo_ready, 1)

            def half_stats(n, half):
                dve.wait_ge(o_done, 2 * n + half + 1)
                dve.bn_stats(hstat[:, half, :], oacc[half][:, :]).then_inc(hstat_ready, 1)

            def partition_moments(n, u, b):
                dve.wait_ge(hstat_ready, 2 * n + 2)
                dve.memset(gate[:, 0:1], 0.0)
                dve.bn_aggr(pstat[:, :], hstat[:, :, :]).then_inc(pstat_ready, 1)
                dve.wait_ge(pstat_ready, n + 1)
                dve.tensor_tensor(mom[:, 0:1], pstat[:, 0:1], cshift[u][:, b:b + 1], ALU.add)\
                    .then_inc(mean_ready, 1)
                dve.wait_ge(mean_ready, n + 1)
                dve.scalar_tensor_tensor(out=mom[:, 1:2], in0=mom[:, 0:1], scalar=mom[:, 0:1],
                                         in1=pstat[:, 1:2], op0=ALU.mult, op1=ALU.add).then_inc(mom_ready, 1)

            def variance(n, u, b):
                dve.wait_ge(stat_done, n + 1)
                dve.tensor_tensor(gmom[:, :], stat[:, 0:2], zero_eps, ALU.add).then_inc(gmom_ready, 1)
                dve.wait_ge(gmom_ready, n + 1)
                dve.scalar_tensor_tensor(out=nvar[:, :], in0=gmom[:, 0:1], scalar=gmom[:, 0:1],
                                         in1=gmom[:, 1:2], op0=ALU.mult, op1=ALU.subtract)\
                    .then_inc(nvar_ready, 1)
                dve.tensor_tensor(cmu[:, :], cshift[u][:, b:b + 1], gmom[:, 0:1], ALU.subtract)
                dve.wait_ge(nvar_ready, n + 1)
                dve.tensor_scalar(var[:, :], nvar[:, :], -1.0, EPS, ALU.mult, ALU.max).then_inc(var_ready, 1)

            def norm_scale(n):
                dve.wait_ge(rstd_ready, n + 1)
                dve.wait_ge(normed, 2 * n + 2)
                dve.tensor_tensor(nscale[:, :], rstd[:, :], col("gn_w"), ALU.mult).then_inc(nscale_ready, 1)
                dve.wait_ge(nscale_ready, n + 1)
                dve.scalar_tensor_tensor(out=nbias[:, :], in0=cmu[:, :], scalar=nscale[:, :], in1=col("gn_b"),
                                         op0=ALU.mult, op1=ALU.add).then_inc(norm_ready, 1)

            def u3_out(p):
                dve.wait_ge(u_done, p + 1)
                for a in range(2):
                    dve.scalar_tensor_tensor(out=u3[:, a, :], in0=w("bk_rows"), scalar=gram[:, a, 2 * C:2 * C + 1],
                                             in1=mid1[:, a * C:(a + 1) * C], op0=ALU.mult, op1=ALU.add)
                for a in range(2):
                    last = dve.scalar_tensor_tensor(out=krow[:, a, :], in0=diag32,
                                                    scalar=mid1[:, 2 * C + a:2 * C + a + 1],
                                                    in1=nbk32[:, :], op0=ALU.mult, op1=ALU.add)
                last.then_inc(u3_ready, 1)

            def shift_scores(p):
                dve.wait_ge(scores_done, p + 1)
                dve.tensor_tensor(sc_m[:, :, :], mid0[:, 0:6 * W32].rearrange("p (i c) -> p i c", c=W32),
                                  other_head.unsqueeze(1).broadcast_to([C, 6, W32]), ALU.add).then_inc(masked, 1)
                dve.wait_ge(masked, p + 1)
                dve.tensor_reduce(smax[:, :], sc_m[:, :, :], AX.X, ALU.max).then_inc(max_ready, 1)
                dve.wait_ge(max_ready, p + 1)
                dve.tensor_tensor(sc_d[:, :, :], sc_m[:, :, :],
                                  smax[:, :].unsqueeze(2).broadcast_to([C, 6, W32]), ALU.subtract)\
                    .then_inc(shifted, 1)

            def softmax_out(p):
                dve.wait_ge(exp_ready, p + 1)
                dve.tensor_reduce(ssum[:, :], probs[:, :, :], AX.X, ALU.add).then_inc(sum_ready, 1)
                dve.tensor_tensor(abv_m[:, :, :], probs[:, 4:6, :], bvr[:, :].unsqueeze(1).broadcast_to([C, 2, W32]),
                                  ALU.mult).then_inc(abv_step, 1)
                dve.wait_ge(sum_ready, p + 1)
                dve.reciprocal(sinv[:, :], ssum[:, :]).then_inc(inv_ready, 1)
                dve.wait_ge(abv_step, 2 * p + 1)
                dve.tensor_reduce(abv_s[:, :], abv_m[:, :, :], AX.X, ALU.add).then_inc(abv_step, 1)
                dve.wait_ge(inv_ready, p + 1)
                for j in range(4):
                    q = slice(W32 * j, W32 * (j + 1))
                    last = dve.tensor_tensor(attn[q, :, q], probs[q, :, :],
                                             sinv[q, :].unsqueeze(2).broadcast_to([W32, 6, W32]), ALU.mult)
                last.then_inc(attn_ready, 1)
                dve.wait_ge(abv_step, 2 * p + 2)
                dve.tensor_tensor(abv[:, :], abv_s[:, :], sinv[:, 4:6], ALU.mult).then_inc(abv_ready, 1)

            def n_out(p, parity):
                dve.wait_ge(m_done, p + 1)
                dve.tensor_tensor(nmat[:, 0:2, :, :].rearrange("p i a c -> p (i a) c"),
                                  mid1[:, :].rearrange("p (i c) -> p i c", c=C),
                                  ident.unsqueeze(1).broadcast_to([C, 4, C]), ALU.add)
                dve.tensor_tensor(nmat[:, 2, :, :], mid0[:, 0:2 * C].rearrange("p (i c) -> p i c", c=C),
                                  ident.unsqueeze(1).broadcast_to([C, 2, C]), ALU.add)
                dve.tensor_scalar(cshift[parity][:, :], mid0[:, 2 * C:2 * C + 2], col("bo"), None, ALU.add)\
                    .then_inc(n_ready, 1)

            def step(h, u, front, middle, back):
                p = 2 * h + u
                for j in range(2 * QT):
                    b, k = divmod(j, QT)
                    n = 4 * h + 2 * u + b - 4
                    if front:
                        low_part(h, u, j)
                    if back and k == 3:
                        norm_scale(n)
                    if back and k < 2:
                        half_stats(n, k)
                    if back and k == 1:
                        partition_moments(n, u, b)
                    if middle:
                        if j == 1:
                            u3_out(p - 1)
                        if j == 3:
                            shift_scores(p - 1)
                        if j == 4:
                            softmax_out(p - 1)
                        if j == 5:
                            dve.wait_ge(z_done, p)
                            dve.tensor_copy(z[:, 2, :, :], mid0[:, 0:2 * C].rearrange("p (i c) -> p i c", c=C))\
                                .then_inc(z3_ready, 1)
                        if j == 6:
                            n_out(p - 1, 1 - u)
                        if j == 7:
                            dve.wait_ge(pqhi_ready, p)
                            dve.tensor_tensor(pq_lo[1 - u][:, :, :, :].rearrange("p a s c -> p (a s c)"), mid1[:, :],
                                              pq_hi[1 - u][:, :, :, :].rearrange("p a s c -> p (a s c)").bitcast(f32),
                                              ALU.subtract).then_inc(pqlo_ready, 1)
                    if back and k == 2:
                        variance(n, u, b)

            steps(dve, step)

        @block.gpsimd
        def _(pool):
            pool.wait_ge(consts_in, 64)

            def step(h, u, front, middle, back):
                for b in range(2):
                    slot = 2 * u + b
                    n = 4 * h + slot
                    if back:
                        pool.wait_ge(var_ready, n - 3)
                        pool.tensor_tensor(rstd[:, :], var[:, :], neg_half, ALU.pow).then_inc(rstd_ready, 1)
                    if front:
                        for s in range(2):
                            pool.wait_ge(split_hi, 2 * n + s + 1)
                            pool.tensor_tensor(xy_lo[slot][:, s, :], raw[slot][:, s, :],
                                               xy_hi[slot][:, s, :].bitcast(f32), ALU.subtract)\
                                .then_inc(split_lo, 1)

            steps(pool, step)


def kernel(**inputs):
    import numpy as np
    import concourse.bacc as _bacc
    from concourse import mybir as _mybir
    from concourse.bass_utils import run_bass_kernel_spmd as _run

    a = {k: np.asarray(v) for k, v in inputs.items()}
    l0 = lambda k: a["L0_xattn_" + k]
    l1 = lambda k: a["L1_xattn_" + k]
    rows = lambda v: np.broadcast_to(v[None, :], (C, C))
    mats = {"kpT": l0("wk_point").T, "qpT": l0("wq_point").T, "kT": l1("Wk").T, "qrT": l0("wq_rgb").T,
            "krT": l0("wk_rgb").T, "qT": l1("Wq").T, "vp": l0("wv_point"), "vr": l0("wv_rgb"),
            "oT": l1("Wo").T, "ppT": l0("proj_p2r").T, "prT": l0("proj_r2p").T, "v": l1("Wv"),
            "bk_rows": rows(l1("bk")), "bq_rows": rows(l1("bq"))}
    weights = np.ascontiguousarray(np.stack([mats[k] for k in WNAMES], axis=1))
    vectors = np.ascontiguousarray(np.stack([l1(k) for k in VNAMES], axis=1))
    bv_rows = np.ascontiguousarray(np.repeat(l1("bv").reshape(C // W32, W32), W32, axis=0))

    ch = np.arange(C)
    head = ch // (C // H)
    w32 = np.arange(W32)
    consts = np.concatenate([
        np.eye(C), head[:, None] == head[None, :], np.full((C, C), 1.0 / C),
        np.where((ch[:, None] % W32) // (C // H) == w32[None, :] // (C // H), 0.0, NEG),
        ch[:, None] % W32 == w32[None, :],
        np.zeros((C, 1)), np.full((C, 1), EPS), np.full((C, 1), -0.5)], axis=1).astype(np.float32)

    nc = _bacc.Bacc("TRN2", target_bir_lowering=False, num_devices=1)
    arrays = {"x": np.ascontiguousarray(a["x"]), "ctx": np.ascontiguousarray(a["ctx_4096"]), "weights": weights,
              "vectors": vectors, "bv_rows": bv_rows, "consts": consts}
    args = [nc.dram_tensor(f"in_{k}", v.shape, _mybir.dt.from_np(v.dtype), kind="ExternalInput").ap()
            for k, v in arrays.items()]
    out = nc.dram_tensor("out", (B, C, N), _mybir.dt.float32, kind="ExternalOutput").ap()
    cross_attention_pair_kernel(nc, *args, out)
    r = _run(nc, [{f"in_{k}": v for k, v in arrays.items()}], core_ids=[0])
    return r.results[0]["out"]
```

```python
import concourse.bass as bass
from concourse import mybir
from concourse.alu_op_type import AluOpType as ALU
from contextlib import ExitStack

B, C, N, H = 32, 128, 1024, 8
EPS = 1e-5
PAIRS = B // 2
CH = N // C
QT = 4
HALF = N // 2
W32 = 32
NEG = -1e30

WNAMES = ["kpT", "qpT", "kT", "qrT", "krT", "qT", "vp", "vr", "oT", "ppT", "prT", "v", "bk_rows", "bq_rows"]
VNAMES = ["bk", "bo", "gn_w", "gn_b"]


def cross_attention_pair_kernel(nc, x, y, weights, vectors, bv_rows, consts, out):
    f32, f32r = mybir.dt.float32, mybir.dt.float32r
    ACT = mybir.ActivationFunctionType
    AX = mybir.AxisListType

    ctx = ExitStack()
    with ctx:
        def sb(name, shape, dt=f32):
            return ctx.enter_context(nc.sbuf_tensor(name, shape, dt))

        def pb(name, shape):
            return ctx.enter_context(nc.psum_tensor(name, shape, f32))

        def sem(name):
            return ctx.enter_context(nc.semaphore(name))

        wt = sb("wt", [C, len(WNAMES), C])
        vec = sb("vec", [C, len(VNAMES)])
        bvr = sb("bvr", [C, W32])
        cst = sb("cst", [C, 3 * C + 2 * W32 + 8])
        ident = cst[:, 0:C]
        same_head = cst[:, C:2 * C]
        mean_w = cst[:, 2 * C:3 * C]
        other_head = cst[:, 3 * C:3 * C + W32]
        diag32 = cst[:, 3 * C + W32:3 * C + 2 * W32]
        k0 = 3 * C + 2 * W32
        zero_eps = cst[:, k0:k0 + 4]
        neg_half = cst[:, k0 + 4:k0 + 6]
        eps2 = cst[:, k0 + 6:k0 + 8]

        def w(name):
            return wt[:, WNAMES.index(name), :]

        def col(name):
            k = VNAMES.index(name)
            return vec[:, k:k + 1]

        bq_head = sb("bq_head", [C, C])
        nbk32 = sb("nbk32", [C, W32])
        raw = [sb(f"raw{n}", [C, 2, N]) for n in range(4)]
        xy_hi = [sb(f"xy_hi{n}", [C, 2, N], f32r) for n in range(4)]
        xy_lo = [sb(f"xy_lo{n}", [C, 2, N], f32r) for n in range(4)]
        t_hi = [sb(f"t_hi{n}", [C, CH, 2 * C + 2], f32r) for n in range(2)]
        t_lo = [sb(f"t_lo{n}", [C, CH, 2 * C], f32r) for n in range(2)]
        gram = sb("gram", [C, 2, 2 * C + 2])
        u12 = sb("u12", [C, 2, 2, C])
        u3 = sb("u3", [C, 2, C])
        krow = sb("krow", [C, 2, W32])
        sc_m = sb("sc_m", [C, 6, W32])
        sc_d = sb("sc_d", [C, 6, W32])
        probs = sb("probs", [C, 6, W32])
        smax = sb("smax", [C, 6])
        ssum = sb("ssum", [C, 6])
        sinv = sb("sinv", [C, 6])
        attn = sb("attn", [C, 6, C])
        abv_m = sb("abv_m", [C, 2, W32])
        abv_s = sb("abv_s", [C, 2])
        abv = sb("abv", [C, 2])
        z = sb("z", [C, 3, 2, C])
        nmat = sb("nmat", [C, 3, 2, C])
        cshift = [sb(f"cshift{n}", [C, 2]) for n in range(2)]
        pq_hi = [sb(f"pq_hi{n}", [C, 2, 2, C], f32r) for n in range(2)]
        pq_lo = [sb(f"pq_lo{n}", [C, 2, 2, C], f32r) for n in range(2)]
        gate = sb("gate", [1, 8])
        hstat = sb("hstat", [C, 2, 2, 6])
        pstat = sb("pstat", [C, 2, 2])
        mom = sb("mom", [C, 2, 2])
        gmom = sb("gmom", [C, 2, 2])
        musq = sb("musq", [C, 2])
        vraw = sb("vraw", [C, 2])
        var = sb("var", [C, 2])
        rstd = sb("rstd", [C, 2])
        cmu = sb("cmu", [C, 2])
        cms = sb("cms", [C, 2])
        nscale = sb("nscale", [C, 2])
        nbias = sb("nbias", [C, 2])
        res = [sb(f"res{n}", [C, N]) for n in range(4)]

        tp = [pb(f"tp{n}", [C, 2, 2 * C]) for n in range(2)]
        gacc = pb("gacc", [C, HALF])
        mid0 = pb("mid0", [C, HALF])
        mid1 = pb("mid1", [C, HALF])
        stat = pb("stat", [C, HALF])
        oacc = [pb(f"oacc{n}", [C, HALF]) for n in range(2)]

        consts_in = sem("consts_in")
        weights_in = sem("weights_in")
        loaded = [sem(f"loaded{n}") for n in range(4)]
        stored = [sem(f"stored{n}") for n in range(4)]
        prepared = sem("prepared")
        attn_zero = sem("attn_zero")
        ones_set = sem("ones_set")
        transposed = sem("transposed")
        thi_ready = sem("thi_ready")
        tlo_ready = sem("tlo_ready")
        gram_done = sem("gram_done")
        gram_ready = sem("gram_ready")
        u_done = sem("u_done")
        u12_ready = sem("u12_ready")
        u3_ready = sem("u3_ready")
        scores_done = sem("scores_done")
        masked = sem("masked")
        max_ready = sem("max_ready")
        shifted = sem("shifted")
        exp_ready = sem("exp_ready")
        sum_ready = sem("sum_ready")
        inv_ready = sem("inv_ready")
        attn_ready = sem("attn_ready")
        abv_step = sem("abv_step")
        abv_ready = sem("abv_ready")
        z_done = sem("z_done")
        z12_ready = sem("z12_ready")
        z3_ready = sem("z3_ready")
        m_done = sem("m_done")
        n_ready = sem("n_ready")
        pq_done = sem("pq_done")
        pqhi_ready = sem("pqhi_ready")
        pqlo_ready = sem("pqlo_ready")
        split_hi = sem("split_hi")
        split_lo = sem("split_lo")
        o_done = sem("o_done")
        o_out = sem("o_out")
        hstat_ready = sem("hstat_ready")
        pstat_ready = sem("pstat_ready")
        mean_ready = sem("mean_ready")
        meansq_ready = sem("meansq_ready")
        mom_ready = sem("mom_ready")
        stat_done = sem("stat_done")
        gmom_ready = sem("gmom_ready")
        musq_ready = sem("musq_ready")
        vraw_ready = sem("vraw_ready")
        var_ready = sem("var_ready")
        rstd_ready = sem("rstd_ready")
        nscale_ready = sem("nscale_ready")
        cms_ready = sem("cms_ready")
        norm_ready = sem("norm_ready")
        normed = sem("normed")

        def steps(eng, step):
            step(0, 0, True, False, False)
            step(0, 1, True, True, False)
            with eng.Fori(1, PAIRS // 2) as i:
                step(i, 0, True, True, True)
                step(i, 1, True, True, True)
            step(PAIRS // 2, 0, False, True, True)
            step(PAIRS // 2, 1, False, False, True)

        block = ctx.enter_context(nc.Block())

        @block.sync
        def _(sp):
            def load(h, u, b):
                n = 2 * u + b
                sp.dma_start(raw[n][:, 0, :], x[4 * h + n]).then_inc(loaded[n], 16)
                sp.dma_start(raw[n][:, 1, :], y[4 * h + n]).then_inc(loaded[n], 16)

            sp.dma_start(cst[:, :], consts).then_inc(consts_in, 16)
            load(0, 0, 0)
            load(0, 0, 1)
            sp.dma_start(wt[:, :, :], weights).then_inc(weights_in, 16)
            sp.dma_start(vec[:, :], vectors).then_inc(weights_in, 16)
            sp.dma_start(bvr[:, :], bv_rows).then_inc(weights_in, 16)
            load(0, 1, 0)
            load(0, 1, 1)

            def step(h, u, front, middle, back, refill=True):
                for b in range(2):
                    n = 4 * h + 2 * u + b
                    if front and refill:
                        sp.wait_ge(split_hi, 2 * n + 2)
                        sp.wait_ge(split_lo, 2 * n + 2)
                        sp.wait_ge(transposed, QT * (n + 1))
                        load(h + 1, u, b)
                for b in range(2):
                    q = 4 * h + 2 * u + b - 4
                    if back:
                        sp.wait_ge(normed, q + 3)
                        sp.dma_start(out[q], res[2 * u + b][:, :]).then_inc(stored[2 * u + b], 16)

            step(0, 0, True, False, False)
            step(0, 1, True, True, False)
            with sp.Fori(1, PAIRS // 2 - 1) as i:
                step(i, 0, True, True, True)
                step(i, 1, True, True, True)
            last = PAIRS // 2 - 1
            step(last, 0, True, True, True, refill=False)
            step(last, 1, True, True, True, refill=False)
            step(last + 1, 0, False, True, True)
            step(last + 1, 1, False, False, True)
            for n in range(4):
                sp.wait_ge(stored[n], 16 * (B // 4 + 1))

        @block.tensor
        def _(pe):
            pe.wait_ge(consts_in, 16)
            pe.wait_ge(ones_set, 2)

            def transposes(h, u, j):
                b, k = divmod(j, QT)
                slot = 2 * u + b
                t = QT * (4 * h + slot) + k
                if k == 0:
                    pe.wait_ge(loaded[slot], 32 * (h + 1))
                if not (isinstance(t, int) and t < 2):
                    pe.wait_ge(tlo_ready, t - 1)
                for c in range(2):
                    for s in range(2):
                        src = raw[slot][:, s, (2 * k + c) * C:(2 * k + c + 1) * C]
                        mm = pe.transpose(tp[k % 2][:, c, s * C:(s + 1) * C], src, ident)
                mm.then_inc(transposed, 1)

            def gram_quarter(h, u, j):
                b, k = divmod(j, QT)
                n = 4 * h + 2 * u + b
                pe.wait_ge(tlo_ready, QT * n + k + 1)
                if k == 0 and not (isinstance(n, int) and n < 1):
                    pe.wait_ge(gram_ready, n)
                for c in range(2 * k, 2 * k + 2):
                    yhi, ylo = t_hi[b][:, c, C:2 * C], t_lo[b][:, c, C:2 * C]
                    pe.matmul(gacc[:, 0:2 * C + 2], yhi, t_hi[b][:, c, :], start=(c == 0), stop=False)
                    pe.matmul(gacc[:, 0:2 * C], yhi, t_lo[b][:, c, :], start=False, stop=False,
                              skip_group_check=True)
                    mm = pe.matmul(gacc[:, 0:2 * C + 2], ylo, t_hi[b][:, c, :], start=False,
                                   stop=(c == CH - 1))
                if k == QT - 1:
                    mm.then_inc(gram_done, 1)

            def out_half(h, u, b, half):
                slot = 2 * u + b
                n = 4 * h + slot
                if half == 0:
                    if b == 0:
                        pe.wait_ge(pqlo_ready, 2 * h + u + 1)
                    pe.wait_ge(split_hi, 2 * n + 2)
                    pe.wait_ge(split_lo, 2 * n + 2)
                pe.wait_ge(o_out, 2 * n + 1 + half)
                cols = slice(half * HALF, (half + 1) * HALF)
                for s in range(2):
                    whi, wlo = pq_hi[u][:, b, s, :], pq_lo[u][:, b, s, :]
                    pe.matmul(oacc[half][:, :], whi, xy_hi[slot][:, s, cols], start=(s == 0), stop=False)
                    pe.matmul(oacc[half][:, :], whi, xy_lo[slot][:, s, cols], start=False, stop=False)
                    mm = pe.matmul(oacc[half][:, :], wlo, xy_hi[slot][:, s, cols], start=False, stop=(s == 1))
                mm.then_inc(o_done, 1)

            def group_moments(p):
                pe.wait_ge(mom_ready, p + 1)
                pe.matmul(stat[:, 0:4], mean_w, mom[:, :, :], start=True, stop=True).then_inc(stat_done, 1)

            def u_products(p):
                if isinstance(p, int) and p == 0:
                    pe.wait_ge(weights_in, 48)
                    pe.wait_ge(prepared, 5)
                pe.wait_ge(gram_ready, 2 * p + 2)
                if not (isinstance(p, int) and p < 1):
                    pe.wait_ge(pqlo_ready, p)
                for a in range(2):
                    pe.matmul(mid0[:, a * 2 * C:(a + 1) * 2 * C], gram[:, a, 0:C], wt[:, 0:2, :],
                              start=True, stop=True)
                for a in range(2):
                    pe.matmul(mid1[:, a * C:(a + 1) * C], gram[:, a, C:2 * C], w("kT"), start=True, stop=True)
                pe.matmul(mid1[:, 2 * C:2 * C + 2], w("kT"), gram[:, :, 2 * C], start=True, stop=True)\
                    .then_inc(u_done, 1)

            def scores(p):
                pe.wait_ge(u12_ready, p + 1)
                pe.wait_ge(u3_ready, p + 1)
                for j in range(4):
                    q = slice(W32 * j, W32 * (j + 1))
                    s1 = mid0[q, 0:2 * W32]
                    pe.matmul(s1, w("qrT")[:, q], u12[:, :, 0, q], start=True, stop=True)
                for j in range(4):
                    q = slice(W32 * j, W32 * (j + 1))
                    s3 = mid0[q, 4 * W32:6 * W32]
                    pe.matmul(s3, w("qT")[:, q], u3[:, :, q], start=True, stop=False)
                for j in range(4):
                    q = slice(W32 * j, W32 * (j + 1))
                    s3 = mid0[q, 4 * W32:6 * W32]
                    pe.matmul(s3, bq_head[:, q], krow[:, :, :], start=False, stop=True)
                for a in range(2):
                    for j in range(4):
                        q = slice(W32 * j, W32 * (j + 1))
                        s2 = mid0[q, (2 + a) * W32:(3 + a) * W32]
                        mm = pe.matmul(s2, u12[:, a, 1, q], w("krT")[:, q], start=True, stop=True)
                mm.then_inc(scores_done, 1)

            def z_products(p):
                pe.wait_ge(attn_ready, p + 1)
                for i, name in enumerate(("vp", "vr", "oT")):
                    for a in range(2):
                        dst = mid1[:, (2 * i + a) * C:(2 * i + a + 1) * C] if i < 2 else mid0[:, a * C:(a + 1) * C]
                        mm = pe.matmul(dst, attn[:, 2 * i + a, :], w(name), start=True, stop=True)
                mm.then_inc(z_done, 1)

            def m_products(p):
                pe.wait_ge(z12_ready, p + 1)
                pe.wait_ge(z3_ready, p + 1)
                pe.matmul(mid1[:, 0:2 * C], w("ppT"), z[:, 0, :, :], start=True, stop=True)
                pe.matmul(mid1[:, 2 * C:4 * C], w("prT"), z[:, 1, :, :], start=True, stop=True)
                pe.matmul(mid0[:, 0:2 * C], w("v"), z[:, 2, :, :], start=True, stop=True)
                pe.wait_ge(abv_ready, p + 1)
                pe.matmul(mid0[:, 2 * C:2 * C + 2], w("oT"), abv[:, :], start=True, stop=True).then_inc(m_done, 1)

            def pq_products(p):
                pe.wait_ge(n_ready, p + 1)
                for a in range(2):
                    for s in range(2):
                        k = 2 * a + s
                        mm = pe.matmul(mid1[:, k * C:(k + 1) * C], nmat[:, 1 - s, a, :], nmat[:, 2, a, :],
                                       start=True, stop=True)
                mm.then_inc(pq_done, 1)

            def step(h, u, front, middle, back):
                p = 2 * h + u
                for j in range(2 * QT):
                    if front:
                        transposes(h, u, j)
                    if back and j < 4:
                        out_half(h - 1, u, j // 2, j % 2)
                    if middle and j == 0:
                        u_products(p - 1)
                    if middle and j == 2:
                        scores(p - 1)
                    if middle and j == 5:
                        z_products(p - 1)
                    if back and j == 6:
                        group_moments(p - 2)
                    if middle and j == 7:
                        pq_products(p - 1)
                    if middle and j == 6:
                        m_products(p - 1)
                    if front and j > 0:
                        gram_quarter(h, u, j - 1)
                if front:
                    gram_quarter(h, u, 2 * QT - 1)

            steps(pe, step)

        @block.scalar
        def _(act):
            def high_part(h, u, j):
                b, k = divmod(j, QT)
                n = 4 * h + 2 * u + b
                act.wait_ge(transposed, QT * n + k + 1)
                if k == 0 and not (isinstance(n, int) and n < 2):
                    act.wait_ge(gram_done, n - 1)
                act.activation(t_hi[b][:, 2 * k:2 * k + 2, 0:2 * C], tp[k % 2][:, :, :], ACT.Copy)\
                    .then_inc(thi_ready, 1)

            def gram_out(h, u, b):
                n = 4 * h + 2 * u + b
                p = 2 * h + u
                act.wait_ge(gram_done, n + 1)
                if b == 0 and not (isinstance(p, int) and p < 1):
                    act.wait_ge(u_done, p)
                    act.wait_ge(u3_ready, p)
                act.activation(gram[:, b, :], gacc[:, 0:2 * C + 2], ACT.Copy).then_inc(gram_ready, 1)

            def split_high(h, u, b, s, back):
                slot = 2 * u + b
                n = 4 * h + slot
                act.wait_ge(loaded[slot], 32 * (h + 1))
                if s == 0 and back:
                    act.wait_ge(o_done, 2 * n - 6)
                act.activation(xy_hi[slot][:, s, :], raw[slot][:, s, :], ACT.Copy).then_inc(split_hi, 1)

            def out_to_sbuf(h, u, b, half):
                n = 4 * h + 2 * u + b
                act.wait_ge(o_done, 2 * n + half + 1)
                if half == 0:
                    act.wait_ge(stored[2 * u + b], 16 * (h + 1))
                act.activation(res[2 * u + b][:, half * HALF:(half + 1) * HALF], oacc[half][:, :], ACT.Copy)\
                    .then_inc(o_out, 1)

            def normalise(h, u, b):
                act.wait_ge(norm_ready, 2 * h + u + 1)
                act.activation(res[2 * u + b][:, :], res[2 * u + b][:, :], ACT.Identity,
                               bias=nbias[:, b:b + 1], scale=nscale[:, b:b + 1]).then_inc(normed, 1)

            def step(h, u, front, middle, back):
                p = 2 * h + u
                for j in range(2 * QT):
                    if front:
                        high_part(h, u, j)
                    if middle and j == 1:
                        act.wait_ge(u_done, p)
                        act.activation(u12[:, :, :, :], mid0[:, :], ACT.Copy).then_inc(u12_ready, 1)
                    if middle and j == 3:
                        act.wait_ge(shifted, p)
                        act.activation(probs[:, :, :], sc_d[:, :, :], ACT.Exp).then_inc(exp_ready, 1)
                    if back and j < 4:
                        out_to_sbuf(h - 1, u, j // 2, j % 2)
                    if front and j == QT:
                        gram_out(h, u, 0)
                    if front and j in (2, 3, 4, 6):
                        split_high(h, u, j // 4, int(j in (3, 6)), back)
                    if middle and j == 5:
                        act.wait_ge(z_done, p)
                        act.activation(z[:, 0:2, :, :], mid1[:, :], ACT.Copy).then_inc(z12_ready, 1)
                    if middle and j == 7:
                        act.wait_ge(pq_done, p)
                        act.activation(pq_hi[1 - u][:, :, :, :], mid1[:, :], ACT.Copy).then_inc(pqhi_ready, 1)
                    if back and j == 7:
                        normalise(h - 1, u, 0)
                    if front and j == 7:
                        gram_out(h, u, 1)
                    if back and j == 7:
                        normalise(h - 1, u, 1)

            steps(act, step)

        @block.vector
        def _(dve):
            dve.memset(t_hi[0][:, :, 2 * C:].bitcast(f32), 1.0).then_inc(ones_set, 1)
            dve.memset(t_hi[1][:, :, 2 * C:].bitcast(f32), 1.0).then_inc(ones_set, 1)
            dve.memset(attn[:, :, :], 0.0).then_inc(attn_zero, 1)
            dve.memset(gate[:, 1:2], 0.0).then_inc(o_out, 2)
            dve.memset(gate[:, 2:3], 0.0).then_inc(normed, 2)
            for n in range(4):
                dve.memset(gate[:, 3 + n:4 + n], 0.0).then_inc(stored[n], 16)
            dve.wait_ge(attn_zero, 1)

            def prepare():
                dve.wait_ge(consts_in, 16)
                dve.wait_ge(weights_in, 48)
                s0, s1 = float(C // H) ** -0.5, float(C) ** -0.5
                dve.tensor_scalar(w("qpT"), w("qpT"), s0, None, ALU.mult).then_inc(prepared, 1)
                dve.tensor_scalar(w("qrT"), w("qrT"), s0, None, ALU.mult).then_inc(prepared, 1)
                dve.tensor_scalar(w("qT"), w("qT"), s1, None, ALU.mult).then_inc(prepared, 1)
                dve.scalar_tensor_tensor(out=bq_head[:, :], in0=w("bq_rows"), scalar=s1, in1=same_head,
                                         op0=ALU.mult, op1=ALU.mult).then_inc(prepared, 1)
                dve.tensor_scalar(nbk32[:, :], diag32, col("bk"), float(N), ALU.mult, ALU.mult)\
                    .then_inc(prepared, 1)
                dve.wait_ge(prepared, 5)

            def low_part(h, u, j):
                b, k = divmod(j, QT)
                t = QT * (4 * h + 2 * u + b) + k
                dve.wait_ge(thi_ready, t + 1)
                dve.tensor_tensor(t_lo[b][:, 2 * k:2 * k + 2, :], tp[k % 2][:, :, :],
                                  t_hi[b][:, 2 * k:2 * k + 2, 0:2 * C].bitcast(f32), ALU.subtract)\
                    .then_inc(tlo_ready, 1)

            def half_stats(n, u, b, half):
                dve.wait_ge(o_out, 2 * n + half + 3)
                dve.bn_stats(hstat[:, b, half, :], res[2 * u + b][:, half * HALF:(half + 1) * HALF])\
                    .then_inc(hstat_ready, 1)

            def partition_moments(p, u):
                dve.wait_ge(hstat_ready, 4 * p + 4)
                dve.memset(gate[:, 0:1], 0.0)
                for b in range(2):
                    dve.bn_aggr(pstat[:, b, :], hstat[:, b, :, :]).then_inc(pstat_ready, 1)
                dve.wait_ge(pstat_ready, 2 * p + 2)
                dve.tensor_tensor(mom[:, 0, :], pstat[:, :, 0], cshift[u][:, :], ALU.add).then_inc(mean_ready, 1)
                dve.wait_ge(mean_ready, p + 1)
                dve.tensor_tensor(musq[:, :], mom[:, 0, :], mom[:, 0, :], ALU.mult).then_inc(meansq_ready, 1)
                dve.wait_ge(meansq_ready, p + 1)
                dve.tensor_tensor(mom[:, 1, :], musq[:, :], pstat[:, :, 1], ALU.add).then_inc(mom_ready, 1)

            def variance(p, u):
                dve.wait_ge(stat_done, p + 1)
                dve.tensor_tensor(gmom[:, :, :], stat[:, 0:4].rearrange("p (m b) -> p m b", b=2),
                                  zero_eps.rearrange("p (m b) -> p m b", b=2), ALU.add).then_inc(gmom_ready, 1)
                dve.wait_ge(gmom_ready, p + 1)
                dve.tensor_tensor(musq[:, :], gmom[:, 0, :], gmom[:, 0, :], ALU.mult).then_inc(musq_ready, 1)
                dve.tensor_tensor(cmu[:, :], cshift[u][:, :], gmom[:, 0, :], ALU.subtract)
                dve.wait_ge(musq_ready, p + 1)
                dve.tensor_tensor(vraw[:, :], gmom[:, 1, :], musq[:, :], ALU.subtract).then_inc(vraw_ready, 1)
                dve.wait_ge(vraw_ready, p + 1)
                dve.tensor_tensor(var[:, :], vraw[:, :], eps2, ALU.max).then_inc(var_ready, 1)

            def norm_scale(p):
                dve.wait_ge(rstd_ready, p + 1)
                dve.wait_ge(normed, 2 * p + 2)
                dve.tensor_scalar(nscale[:, :], rstd[:, :], col("gn_w"), None, ALU.mult).then_inc(nscale_ready, 1)
                dve.wait_ge(nscale_ready, p + 1)
                dve.tensor_tensor(cms[:, :], cmu[:, :], nscale[:, :], ALU.mult).then_inc(cms_ready, 1)
                dve.wait_ge(cms_ready, p + 1)
                dve.tensor_scalar(nbias[:, :], cms[:, :], col("gn_b"), None, ALU.add).then_inc(norm_ready, 1)

            def u3_out(p):
                dve.wait_ge(u_done, p + 1)
                for a in range(2):
                    dve.scalar_tensor_tensor(out=u3[:, a, :], in0=w("bk_rows"), scalar=gram[:, a, 2 * C:2 * C + 1],
                                             in1=mid1[:, a * C:(a + 1) * C], op0=ALU.mult, op1=ALU.add)
                for a in range(2):
                    last = dve.scalar_tensor_tensor(out=krow[:, a, :], in0=diag32,
                                                    scalar=mid1[:, 2 * C + a:2 * C + a + 1],
                                                    in1=nbk32[:, :], op0=ALU.mult, op1=ALU.add)
                last.then_inc(u3_ready, 1)

            def shift_scores(p):
                dve.wait_ge(scores_done, p + 1)
                dve.tensor_tensor(sc_m[:, :, :], mid0[:, 0:6 * W32].rearrange("p (i c) -> p i c", c=W32),
                                  other_head.unsqueeze(1).broadcast_to([C, 6, W32]), ALU.add).then_inc(masked, 1)
                dve.wait_ge(masked, p + 1)
                dve.tensor_reduce(smax[:, :], sc_m[:, :, :], AX.X, ALU.max).then_inc(max_ready, 1)
                dve.wait_ge(max_ready, p + 1)
                dve.tensor_tensor(sc_d[:, :, :], sc_m[:, :, :],
                                  smax[:, :].unsqueeze(2).broadcast_to([C, 6, W32]), ALU.subtract)\
                    .then_inc(shifted, 1)

            def softmax_out(p):
                dve.wait_ge(exp_ready, p + 1)
                dve.tensor_reduce(ssum[:, :], probs[:, :, :], AX.X, ALU.add).then_inc(sum_ready, 1)
                dve.tensor_tensor(abv_m[:, :, :], probs[:, 4:6, :], bvr[:, :].unsqueeze(1).broadcast_to([C, 2, W32]),
                                  ALU.mult).then_inc(abv_step, 1)
                dve.wait_ge(sum_ready, p + 1)
                dve.reciprocal(sinv[:, :], ssum[:, :]).then_inc(inv_ready, 1)
                dve.wait_ge(abv_step, 2 * p + 1)
                dve.tensor_reduce(abv_s[:, :], abv_m[:, :, :], AX.X, ALU.add).then_inc(abv_step, 1)
                dve.wait_ge(inv_ready, p + 1)
                for j in range(4):
                    q = slice(W32 * j, W32 * (j + 1))
                    last = dve.tensor_tensor(attn[q, :, q], probs[q, :, :],
                                             sinv[q, :].unsqueeze(2).broadcast_to([W32, 6, W32]), ALU.mult)
                last.then_inc(attn_ready, 1)
                dve.wait_ge(abv_step, 2 * p + 2)
                dve.tensor_tensor(abv[:, :], abv_s[:, :], sinv[:, 4:6], ALU.mult).then_inc(abv_ready, 1)

            def n_out(p, parity):
                dve.wait_ge(m_done, p + 1)
                dve.tensor_tensor(nmat[:, 0:2, :, :].rearrange("p i a c -> p (i a) c"),
                                  mid1[:, :].rearrange("p (i c) -> p i c", c=C),
                                  ident.unsqueeze(1).broadcast_to([C, 4, C]), ALU.add)
                dve.tensor_tensor(nmat[:, 2, :, :], mid0[:, 0:2 * C].rearrange("p (i c) -> p i c", c=C),
                                  ident.unsqueeze(1).broadcast_to([C, 2, C]), ALU.add)
                dve.tensor_scalar(cshift[parity][:, :], mid0[:, 2 * C:2 * C + 2], col("bo"), None, ALU.add)\
                    .then_inc(n_ready, 1)

            def step(h, u, front, middle, back):
                p = 2 * h + u
                for j in range(2 * QT):
                    if front:
                        low_part(h, u, j)
                    if front and not middle and j == 6:
                        prepare()
                    if middle and j == 1:
                        u3_out(p - 1)
                    if middle and j == 3:
                        softmax_out(p - 1)
                    if back and j < 4:
                        half_stats(4 * h + 2 * u + j // 2 - 4, u, j // 2, j % 2)
                    if middle and j == 2:
                        shift_scores(p - 1)
                    if back and j == 4:
                        partition_moments(p - 2, u)
                    if middle and j == 5:
                        dve.wait_ge(z_done, p)
                        dve.tensor_copy(z[:, 2, :, :], mid0[:, 0:2 * C].rearrange("p (i c) -> p i c", c=C))\
                            .then_inc(z3_ready, 1)
                    if back and j == 7:
                        norm_scale(p - 2)
                    if middle and j == 6:
                        n_out(p - 1, 1 - u)
                    if back and j == 6:
                        variance(p - 2, u)
                    if middle and j == 7:
                        dve.wait_ge(pqhi_ready, p)
                        dve.tensor_tensor(pq_lo[1 - u][:, :, :, :].rearrange("p a s c -> p (a s c)"), mid1[:, :],
                                          pq_hi[1 - u][:, :, :, :].rearrange("p a s c -> p (a s c)").bitcast(f32),
                                          ALU.subtract).then_inc(pqlo_ready, 1)

            steps(dve, step)

        @block.gpsimd
        def _(pool):
            pool.wait_ge(consts_in, 16)

            def split_low(h, u, b):
                slot = 2 * u + b
                for s in range(2):
                    pool.wait_ge(split_hi, 2 * (4 * h + slot) + s + 1)
                    for c in range(2):
                        cols = slice(c * HALF, (c + 1) * HALF)
                        piece = pool.tensor_tensor(xy_lo[slot][:, s, cols], raw[slot][:, s, cols],
                                                   xy_hi[slot][:, s, cols].bitcast(f32), ALU.subtract)
                    piece.then_inc(split_lo, 1)

            def step(h, u, front, middle, back):
                if front:
                    split_low(h, u, 0)
                if back:
                    pool.wait_ge(var_ready, 2 * h + u - 1)
                    pool.tensor_tensor(rstd[:, :], var[:, :], neg_half, ALU.pow).then_inc(rstd_ready, 1)
                if front:
                    split_low(h, u, 1)

            steps(pool, step)


def kernel(**inputs):
    import numpy as np
    import concourse.bacc as _bacc
    from concourse import mybir as _mybir
    from concourse.bass_utils import run_bass_kernel_spmd as _run

    a = {k: np.asarray(v) for k, v in inputs.items()}
    l0 = lambda k: a["L0_xattn_" + k]
    l1 = lambda k: a["L1_xattn_" + k]
    rows = lambda v: np.broadcast_to(v[None, :], (C, C))
    mats = {"kpT": l0("wk_point").T, "qpT": l0("wq_point").T, "kT": l1("Wk").T, "qrT": l0("wq_rgb").T,
            "krT": l0("wk_rgb").T, "qT": l1("Wq").T, "vp": l0("wv_point"), "vr": l0("wv_rgb"),
            "oT": l1("Wo").T, "ppT": l0("proj_p2r").T, "prT": l0("proj_r2p").T, "v": l1("Wv"),
            "bk_rows": rows(l1("bk")), "bq_rows": rows(l1("bq"))}
    weights = np.ascontiguousarray(np.stack([mats[k] for k in WNAMES], axis=1))
    vectors = np.ascontiguousarray(np.stack([l1(k) for k in VNAMES], axis=1))
    bv_rows = np.ascontiguousarray(np.repeat(l1("bv").reshape(C // W32, W32), W32, axis=0))

    ch = np.arange(C)
    head = ch // (C // H)
    w32 = np.arange(W32)
    consts = np.concatenate([
        np.eye(C), head[:, None] == head[None, :], np.full((C, C), 1.0 / C),
        np.where((ch[:, None] % W32) // (C // H) == w32[None, :] // (C // H), 0.0, NEG),
        ch[:, None] % W32 == w32[None, :],
        np.zeros((C, 2)), np.full((C, 2), EPS), np.full((C, 2), -0.5), np.full((C, 2), EPS)], axis=1).astype(np.float32)

    nc = _bacc.Bacc("TRN2", target_bir_lowering=False, num_devices=1)
    arrays = {"x": np.ascontiguousarray(a["x"]), "ctx": np.ascontiguousarray(a["ctx_4096"]), "weights": weights,
              "vectors": vectors, "bv_rows": bv_rows, "consts": consts}
    args = [nc.dram_tensor(f"in_{k}", v.shape, _mybir.dt.from_np(v.dtype), kind="ExternalInput").ap()
            for k, v in arrays.items()]
    out = nc.dram_tensor("out", (B, C, N), _mybir.dt.float32, kind="ExternalOutput").ap()
    cross_attention_pair_kernel(nc, *args, out)
    r = _run(nc, [{f"in_{k}": v for k, v in arrays.items()}], core_ids=[0])
    return r.results[0]["out"]
```

```python
import concourse.bass as bass
from concourse import mybir
from concourse.alu_op_type import AluOpType as ALU
from contextlib import ExitStack

B, C, N, H = 32, 128, 1024, 8
EPS = 1e-5
PAIRS = B // 2
CH = N // C
HC = CH // 2
HALF = N // 2
QUADS = 4
W32 = 32
DVE_QUADS = 1
LAST_DVE_QUADS = 3
PIECES = 4
WARM = 2
NEG = -1e30

WNAMES = ["kpT", "qpT", "kT", "qrT", "krT", "qT", "vp", "vr", "oT", "ppT", "prT", "v", "bk_rows", "bq_rows"]
VNAMES = ["bq", "bo", "gn_w", "gn_b"]


def cross_attention_pair_kernel(nc, x, y, weights, vectors, quad_rows, consts, out):
    f32, f32r = mybir.dt.float32, mybir.dt.float32r
    ACT = mybir.ActivationFunctionType
    AX = mybir.AxisListType

    ctx = ExitStack()
    with ctx:
        def sb(name, shape, dt=f32):
            return ctx.enter_context(nc.sbuf_tensor(name, shape, dt))

        def pb(name, shape):
            return ctx.enter_context(nc.psum_tensor(name, shape, f32))

        def sem(name):
            return ctx.enter_context(nc.semaphore(name))

        wt = sb("wt", [C, len(WNAMES), C])
        vec = sb("vec", [C, len(VNAMES)])
        quad = sb("quad", [C, 2, W32])
        bk32, bv32 = quad[:, 0, :], quad[:, 1, :]
        cst = sb("cst", [C, 2 * C + W32 + 6])
        ident = cst[:, 0:C]
        mean_w = cst[:, C:2 * C]
        other_head = cst[:, 2 * C:2 * C + W32]
        k0 = 2 * C + W32
        zero_eps = cst[:, k0:k0 + 4]
        neg_half = cst[:, k0 + 4:k0 + 6]

        def w(name):
            return wt[:, WNAMES.index(name), :]

        def col(name):
            k = VNAMES.index(name)
            return vec[:, k:k + 1]

        nbq = sb("nbq", [C, 1])
        mask6 = sb("mask6", [C, 6, W32])
        raw = [sb(f"raw{n}", [C, 2, N]) for n in range(4)]
        y_blocks = [sb(f"y_blocks{n}", [C, QUADS, N // QUADS]) for n in range(4)]
        xy_hi = [sb(f"xy_hi{n}", [C, 2, N], f32r) for n in range(4)]
        xy_lo = [sb(f"xy_lo{n}", [C, 2, N], f32r) for n in range(4)]
        t_hi = [sb(f"t_hi{n}", [C, CH, 2 * C + 2], f32r) for n in range(2)]
        t_lo = [sb(f"t_lo{n}", [C, CH, 2 * C], f32r) for n in range(2)]
        gram = sb("gram", [C, 2, 2 * C + 2])
        k_hi = sb("k_hi", [C, 2, C], f32r)
        k_lo = sb("k_lo", [C, 2, C], f32r)
        wk_hi = sb("wk_hi", [C, 2, C], f32r)
        wk_lo = sb("wk_lo", [C, 2, C], f32r)
        u12 = sb("u12", [C, 2, 2, C])
        u3 = sb("u3", [C, 2, C])
        sk = sb("sk", [C, 2, C])
        sc_m = sb("sc_m", [C, 6, W32])
        sc_d = sb("sc_d", [C, 6, W32])
        probs = sb("probs", [C, 6, W32])
        smax = sb("smax", [C, 6])
        ssum = sb("ssum", [C, 6])
        sinv = sb("sinv", [C, 6])
        attn = sb("attn", [C, 6, C])
        abv_m = sb("abv_m", [C, 2, W32])
        abv_s = sb("abv_s", [C, 2])
        abv = sb("abv", [C, 2])
        z = sb("z", [C, 3, 2, C])
        nmat = sb("nmat", [C, 3, 2, C])
        cshift = [sb(f"cshift{n}", [C, 2]) for n in range(2)]
        pq_hi = [sb(f"pq_hi{n}", [C, 2, 2, C], f32r) for n in range(2)]
        pq_lo = [sb(f"pq_lo{n}", [C, 2, 2, C], f32r) for n in range(2)]
        gate = sb("gate", [1, 8])
        hstat = sb("hstat", [C, 2, 2, 6])
        pstat = sb("pstat", [C, 2, 2])
        mom = sb("mom", [C, 2, 2])
        gmom = sb("gmom", [C, 2, 2])
        neg_var = sb("neg_var", [C, 2])
        var = sb("var", [C, 2])
        rstd = sb("rstd", [C, 2])
        cmu = sb("cmu", [C, 2])
        nscale = sb("nscale", [C, 2])
        nbias = sb("nbias", [C, 2])
        res = [sb(f"res{n}", [C, N]) for n in range(4)]

        tpx = pb("tpx", [C, HC, C])
        tpy = pb("tpy", [C, HC, C])
        gacc = pb("gacc", [C, HALF])
        mid0 = pb("mid0", [C, HALF])
        mid1 = pb("mid1", [C, HALF])
        stat = pb("stat", [C, HALF])
        stat_mb = stat[:, 0:4].rearrange("p (m b) -> p m b", b=2)
        oacc = [pb(f"oacc{n}", [C, HALF]) for n in range(2)]
        o_last = [oacc, [gacc, mid1]]

        consts_in = sem("consts_in")
        weights_in = sem("weights_in")
        x_in = [sem(f"x_in{n}") for n in range(4)]
        y_in = [sem(f"y_in{n}") for n in range(4)]
        blocks_in = [sem(f"blocks_in{n}") for n in range(4)]
        stored = [sem(f"stored{n}") for n in range(4)]
        prepared = sem("prepared")
        attn_zero = sem("attn_zero")
        ones_set = sem("ones_set")
        x_transposed = sem("x_transposed")
        y_transposed = sem("y_transposed")
        xhi_ready = sem("xhi_ready")
        yhi_ready = sem("yhi_ready")
        xlo_ready = sem("xlo_ready")
        ylo_ready = sem("ylo_ready")
        gram_done = sem("gram_done")
        gram_ready = sem("gram_ready")
        wkhi_ready = sem("wkhi_ready")
        khi_ready = sem("khi_ready")
        klo_ready = sem("klo_ready")
        u12_done = sem("u12_done")
        u3_done = sem("u3_done")
        u12_ready = sem("u12_ready")
        u3_ready = sem("u3_ready")
        sk_ready = sem("sk_ready")
        scores_done = sem("scores_done")
        masked = sem("masked")
        max_ready = sem("max_ready")
        shifted = sem("shifted")
        exp_ready = sem("exp_ready")
        sum_ready = sem("sum_ready")
        inv_ready = sem("inv_ready")
        attn_dve_ready = sem("attn_dve_ready")
        attn_pool_ready = sem("attn_pool_ready")
        abv_step = sem("abv_step")
        abv_ready = sem("abv_ready")
        z_done = sem("z_done")
        z12_ready = sem("z12_ready")
        z3_ready = sem("z3_ready")
        m12_done = sem("m12_done")
        m3_done = sem("m3_done")
        wo_abv_done = sem("wo_abv_done")
        n_ready = sem("n_ready")
        c_ready = sem("c_ready")
        pq_done = sem("pq_done")
        pqhi_ready = sem("pqhi_ready")
        pqlo_ready = sem("pqlo_ready")
        split_hi = sem("split_hi")
        split_lo = sem("split_lo")
        o_done = sem("o_done")
        o_out = sem("o_out")
        hstat_ready = sem("hstat_ready")
        pstat_ready = sem("pstat_ready")
        mean_ready = sem("mean_ready")
        mom_ready = sem("mom_ready")
        stat_done = sem("stat_done")
        gmom_ready = sem("gmom_ready")
        neg_var_ready = sem("neg_var_ready")
        var_ready = sem("var_ready")
        rstd_ready = sem("rstd_ready")
        nscale_ready = sem("nscale_ready")
        norm_ready = sem("norm_ready")
        normed = sem("normed")
        last_normed = sem("last_normed")

        def steps(eng, step):
            step(0, 0, True, False, False)
            step(0, 1, True, True, False)
            with eng.Fori(1, PAIRS // 2) as i:
                step(i, 0, True, True, True)
                step(i, 1, True, True, True)
            step(PAIRS // 2, 0, False, True, True)
            step(PAIRS // 2, 1, False, False, True)

        BOTH = slice(0, 2)

        block = ctx.enter_context(nc.Block())

        @block.sync
        def _(sp):
            def load_x(h, n):
                sp.dma_start(raw[n][:, 0, :], x[4 * h + n]).then_inc(x_in[n], 16)

            def load_y_blocks(h, n):
                blocks = y[4 * h + n].rearrange("(i c) (a m) -> i a c m", c=W32, a=QUADS)
                for i in range(QUADS):
                    sp.dma_start(y_blocks[n][:, i, :], blocks[i]).then_inc(blocks_in[n], 16)

            def load_y(h, n):
                sp.dma_start(raw[n][:, 1, :], y[4 * h + n]).then_inc(y_in[n], 16)

            load_x(0, 0)
            sp.dma_start(cst[:, :], consts).then_inc(consts_in, 16)
            load_y_blocks(0, 0)
            load_x(0, 1)
            load_y_blocks(0, 1)
            load_y(0, 0)
            sp.dma_start(vec[:, :], vectors).then_inc(weights_in, 16)
            sp.dma_start(quad[:, :, :], quad_rows).then_inc(weights_in, 16)
            sp.dma_start(wt[:, :, :], weights).then_inc(weights_in, 16)
            load_x(0, 2)
            load_y_blocks(0, 2)
            load_y(0, 1)
            load_x(0, 3)
            load_y_blocks(0, 3)
            load_y(0, 2)
            load_y(0, 3)

            def step(h, u, front, middle, back, refill=True):
                for b in range(2):
                    n = 4 * h + 2 * u + b
                    if front and refill:
                        sp.wait_ge(split_hi, 2 * n + 2)
                        sp.wait_ge(split_lo, 2 * n + 2)
                        sp.wait_ge(x_transposed, 2 * n + 2)
                        sp.wait_ge(y_transposed, 2 * n + 2)
                        load_x(h + 1, 2 * u + b)
                        load_y_blocks(h + 1, 2 * u + b)
                        load_y(h + 1, 2 * u + b)
                for b in range(2):
                    q = 4 * h + 2 * u + b - 4
                    if back:
                        if front:
                            sp.wait_ge(normed, q + 3)
                        elif middle:
                            sp.wait_ge((normed, last_normed)[b], (q + 3, 1)[b])
                        else:
                            sp.wait_ge(normed, q + 2)
                            if b == 1:
                                sp.wait_ge(last_normed, 2)
                        sp.dma_start(out[q], res[2 * u + b][:, :]).then_inc(stored[2 * u + b], 16)

            step(0, 0, True, False, False)
            step(0, 1, True, True, False)
            with sp.Fori(1, PAIRS // 2 - 1) as i:
                step(i, 0, True, True, True)
                step(i, 1, True, True, True)
            last = PAIRS // 2 - 1
            step(last, 0, True, True, True, refill=False)
            step(last, 1, True, True, True, refill=False)
            step(last + 1, 0, False, True, True)
            step(last + 1, 1, False, False, True)
            for n in range(4):
                sp.wait_ge(stored[n], 16 * (B // 4 + 1))

        @block.tensor
        def _(pe):
            def warm_up():
                for k in range(WARM):
                    pe.matmul(oacc[0][:, 0:3 * C], attn[:, 0, :], attn[:, 1:4, :], start=True, stop=True)

            pe.wait_ge(attn_zero, 1)
            warm_up()
            pe.wait_ge(consts_in, 16)
            pe.wait_ge(ones_set, 2)

            def x_transpose(h, u, b, i):
                slot = 2 * u + b
                t = 2 * (4 * h + slot) + i
                if i == 0:
                    pe.wait_ge(x_in[slot], 16 * (h + 1))
                if not (isinstance(t, int) and t < 1):
                    pe.wait_ge(xlo_ready, t)
                chunks = raw[slot][:, 0, :].rearrange("c (r m) -> c m r", m=CH)
                for c in range(HC):
                    mm = pe.transpose(tpx[:, c, :], chunks[:, HC * i + c], ident)
                mm.then_inc(x_transposed, 1)

            def gram_chunks(h, u, b, begin, end):
                n = 4 * h + 2 * u + b
                if begin % HC == 0:
                    pe.wait_ge(xlo_ready, 2 * n + begin // HC + 1)
                    pe.wait_ge(ylo_ready, 2 * n + begin // HC + 1)
                if begin == 0 and not (isinstance(n, int) and n < 1):
                    pe.wait_ge(gram_ready, n)
                for c in range(begin, end):
                    yhi, ylo = t_hi[b][:, c, C:2 * C], t_lo[b][:, c, C:2 * C]
                    pe.matmul(gacc[:, 0:2 * C + 2], yhi, t_hi[b][:, c, :], start=(c == 0), stop=False)
                    pe.matmul(gacc[:, 0:2 * C], yhi, t_lo[b][:, c, :], start=False, stop=False,
                              skip_group_check=True)
                    mm = pe.matmul(gacc[:, 0:2 * C + 2], ylo, t_hi[b][:, c, :], start=False,
                                   stop=(c == CH - 1))
                if end == CH:
                    mm.then_inc(gram_done, 1)

            def out_half(h, u, b, half, last=False):
                bank = o_last[b][half] if last else oacc[half]
                slot = 2 * u + b
                n = 4 * h + slot
                if half == 0:
                    if b == 0:
                        pe.wait_ge(pqhi_ready, 2 * h + u + 1)
                    pe.wait_ge(split_hi, 2 * n + 2)
                    pe.wait_ge(split_lo, 2 * n + 2)
                if not (last and b == 1):
                    pe.wait_ge(o_out, 2 * n + 1 + half)
                cols = slice(half * HALF, (half + 1) * HALF)
                for s in range(2):
                    whi = pq_hi[u][:, b, s, :]
                    pe.matmul(bank[:, :], whi, xy_hi[slot][:, s, cols], start=(s == 0), stop=False)
                    pe.matmul(bank[:, :], whi, xy_lo[slot][:, s, cols], start=False, stop=False)
                if half == 0 and b == 0:
                    pe.wait_ge(pqlo_ready, 2 * h + u + 1)
                for s in range(2):
                    mm = pe.matmul(bank[:, :], pq_lo[u][:, b, s, :], xy_hi[slot][:, s, cols],
                                   start=False, stop=(s == 1))
                mm.then_inc(o_done, 1)

            def group_moments(p, bs=BOTH):
                pe.wait_ge(mom_ready, p + 1 + bs.start)
                pe.matmul(stat_mb[:, :, bs], mean_w, mom[:, :, bs], start=True, stop=True).then_inc(stat_done, 1)

            def u_products(p):
                if isinstance(p, int) and p == 0:
                    pe.wait_ge(weights_in, 48)
                    pe.wait_ge(prepared, 7)
                pe.wait_ge(khi_ready, p + 1)
                if not (isinstance(p, int) and p < 1):
                    pe.wait_ge(pqlo_ready, p)
                    pe.wait_ge(c_ready, p)
                for a in range(2):
                    dst = mid0[:, a * 2 * C:(a + 1) * 2 * C]
                    pe.matmul(dst, k_hi[:, a, :], wk_hi[:, :, :], start=True, stop=False)
                    pe.matmul(dst, k_hi[:, a, :], wk_lo[:, :, :], start=False, stop=False)
                    if a == 0:
                        pe.wait_ge(klo_ready, p + 1)
                    mm = pe.matmul(dst, k_lo[:, a, :], wk_hi[:, :, :], start=False, stop=True)
                mm.then_inc(u12_done, 1)
                for a in range(2):
                    mm = pe.matmul(mid1[:, a * C:(a + 1) * C], gram[:, a, C:2 * C], w("kT"), start=True, stop=True)
                mm.then_inc(u3_done, 1)

            def scores(p):
                pe.wait_ge(u12_ready, p + 1)
                pe.wait_ge(u3_ready, p + 1)
                for j in range(4):
                    q = slice(W32 * j, W32 * (j + 1))
                    s1 = mid0[q, 0:2 * W32]
                    pe.matmul(s1, w("qrT")[:, q], u12[:, :, 0, q], start=True, stop=True)
                for a in range(2):
                    for j in range(4):
                        q = slice(W32 * j, W32 * (j + 1))
                        s2 = mid0[q, (2 + a) * W32:(3 + a) * W32]
                        pe.matmul(s2, u12[:, a, 1, q], w("krT")[:, q], start=True, stop=True)
                for j in range(4):
                    q = slice(W32 * j, W32 * (j + 1))
                    s3 = mid0[q, 4 * W32:6 * W32]
                    pe.matmul(s3, w("qT")[:, q], u3[:, :, q], start=True, stop=False)
                pe.wait_ge(sk_ready, p + 1)
                for j in range(4):
                    q = slice(W32 * j, W32 * (j + 1))
                    s3 = mid0[q, 4 * W32:6 * W32]
                    mm = pe.matmul(s3, w("bq_rows")[:, q], sk[:, :, q], start=False, stop=True)
                mm.then_inc(scores_done, 1)

            def z_products(p):
                pe.wait_ge(attn_dve_ready, p + 1)
                pe.wait_ge(attn_pool_ready, p + 1)
                for i, name in enumerate(("vp", "vr", "oT")):
                    for a in range(2):
                        dst = mid1[:, (2 * i + a) * C:(2 * i + a + 1) * C] if i < 2 else mid0[:, a * C:(a + 1) * C]
                        mm = pe.matmul(dst, attn[:, 2 * i + a, :], w(name), start=True, stop=True)
                mm.then_inc(z_done, 1)

            def m_products(p):
                pe.wait_ge(z12_ready, p + 1)
                pe.matmul(mid1[:, 0:2 * C], w("ppT"), z[:, 0, :, :], start=True, stop=True)
                pe.matmul(mid1[:, 2 * C:4 * C], w("prT"), z[:, 1, :, :], start=True, stop=True).then_inc(m12_done, 1)
                pe.wait_ge(z3_ready, p + 1)
                pe.matmul(mid0[:, 0:2 * C], w("v"), z[:, 2, :, :], start=True, stop=True).then_inc(m3_done, 1)
                pe.wait_ge(abv_ready, p + 1)
                pe.matmul(mid0[:, 2 * C:2 * C + 2], w("oT"), abv[:, :], start=True, stop=True)\
                    .then_inc(wo_abv_done, 1)

            def pq_products(p):
                pe.wait_ge(n_ready, p + 1)
                for a in range(2):
                    for s in range(2):
                        k = 2 * a + s
                        mm = pe.matmul(mid1[:, k * C:(k + 1) * C], nmat[:, 1 - s, a, :], nmat[:, 2, a, :],
                                       start=True, stop=True)
                mm.then_inc(pq_done, 1)

            def step(h, u, front, middle, back):
                p = 2 * h + u
                if front:
                    x_transpose(h, u, 0, 0)
                if front and not middle:
                    warm_up()
                if back and (front or middle):
                    out_half(h - 1, u, 0, 0)
                if middle:
                    u_products(p - 1)
                if back and (front or middle):
                    out_half(h - 1, u, 0, 1)
                if front:
                    x_transpose(h, u, 0, 1)
                if middle:
                    scores(p - 1)
                if front:
                    gram_chunks(h, u, 0, 0, 2)
                if back and (front or middle):
                    out_half(h - 1, u, 1, 0)
                if front:
                    x_transpose(h, u, 1, 0)
                if back and (front or middle):
                    out_half(h - 1, u, 1, 1)
                if front:
                    gram_chunks(h, u, 0, 2, 4)
                    gram_chunks(h, u, 0, 4, 7)
                if middle:
                    z_products(p - 1)
                if front:
                    x_transpose(h, u, 1, 1)
                    gram_chunks(h, u, 0, 7, 8)
                if back and (front or middle):
                    group_moments(p - 2)
                if middle:
                    m_products(p - 1)
                if front:
                    gram_chunks(h, u, 1, 0, 4)
                if middle:
                    pq_products(p - 1)
                if front:
                    gram_chunks(h, u, 1, 4, 8)
                if back and not front and not middle:
                    out_half(h - 1, u, 0, 0, True)
                    out_half(h - 1, u, 0, 1, True)
                    out_half(h - 1, u, 1, 0, True)
                    group_moments(p - 2, slice(0, 1))
                    out_half(h - 1, u, 1, 1, True)
                    group_moments(p - 2, slice(1, 2))

            steps(pe, step)

        @block.scalar
        def _(act):
            def high_part(h, u, b, i, s):
                n = 4 * h + 2 * u + b
                act.wait_ge((x_transposed, y_transposed)[s], 2 * n + i + 1)
                if i == 0 and s == 0 and not (isinstance(n, int) and n < 2):
                    act.wait_ge(gram_done, n - 1)
                act.activation(t_hi[b][:, HC * i:HC * (i + 1), s * C:(s + 1) * C], (tpx, tpy)[s][:, :, :], ACT.Copy)\
                    .then_inc((xhi_ready, yhi_ready)[s], 1)

            def u12_out(p):
                act.wait_ge(u12_done, p + 1)
                act.activation(u12[:, :, :, :], mid0[:, :], ACT.Copy).then_inc(u12_ready, 1)

            def exponent(p):
                act.wait_ge(shifted, p + 1)
                act.activation(probs[:, :, :], sc_d[:, :, :], ACT.Exp).then_inc(exp_ready, 1)

            def z_out(p):
                act.wait_ge(z_done, p + 1)
                act.activation(z[:, 0:2, :, :], mid1[:, :], ACT.Copy).then_inc(z12_ready, 1)
                act.activation(z[:, 2, :, :], mid0[:, 0:2 * C], ACT.Copy).then_inc(z3_ready, 1)

            def pq_high(p, parity):
                act.wait_ge(pq_done, p + 1)
                act.activation(pq_hi[parity][:, :, :, :], mid1[:, :], ACT.Copy).then_inc(pqhi_ready, 1)

            def gram_out(p, b):
                n = 2 * p + b
                act.wait_ge(gram_done, n + 1)
                if b == 0 and not (isinstance(p, int) and p < 1):
                    act.wait_ge(u3_done, p)
                    act.wait_ge(u3_ready, p)
                    act.wait_ge(sk_ready, p)
                    act.wait_ge(klo_ready, p)
                act.activation(gram[:, b, :], gacc[:, 0:2 * C + 2], ACT.Copy).then_inc(gram_ready, 1)

            def split_high(h, u, b, s, back):
                slot = 2 * u + b
                n = 4 * h + slot
                act.wait_ge((x_in, y_in)[s][slot], 16 * (h + 1))
                if s == 0 and back:
                    act.wait_ge(o_done, 2 * n - 6)
                act.activation(xy_hi[slot][:, s, :], raw[slot][:, s, :], ACT.Copy).then_inc(split_hi, 1)

            def out_to_sbuf(h, u, b, half):
                n = 4 * h + 2 * u + b
                act.wait_ge(o_done, 2 * n + half + 1)
                if half == 0:
                    act.wait_ge(stored[2 * u + b], 16 * (h + 1))
                act.activation(res[2 * u + b][:, half * HALF:(half + 1) * HALF], oacc[half][:, :], ACT.Copy)\
                    .then_inc(o_out, 1)

            def normalise_last(h, u, b, halves):
                act.wait_ge(norm_ready, 2 * h + u + 1 + b)
                act.wait_ge(stored[2 * u + b], 16 * (h + 1))
                for half in halves:
                    last = act.activation(res[2 * u + b][:, half * HALF:(half + 1) * HALF], o_last[b][half][:, :],
                                          ACT.Identity, bias=nbias[:, b:b + 1], scale=nscale[:, b:b + 1])
                last.then_inc(normed, 1)

            def normalise(h, u, b):
                act.wait_ge(norm_ready, 2 * h + u + 1)
                act.activation(res[2 * u + b][:, :], res[2 * u + b][:, :], ACT.Identity,
                               bias=nbias[:, b:b + 1], scale=nscale[:, b:b + 1]).then_inc(normed, 1)

            def step(h, u, front, middle, back):
                p = 2 * h + u
                if front:
                    high_part(h, u, 0, 0, 0)
                    high_part(h, u, 0, 0, 1)
                if middle and not front:
                    u12_out(p - 1)
                if back and (front or middle):
                    out_to_sbuf(h - 1, u, 0, 0)
                if front and middle:
                    u12_out(p - 1)
                if middle and front and not back:
                    split_high(h, 0, 1, 1, False)
                if back and (front or middle):
                    out_to_sbuf(h - 1, u, 0, 1)
                if front:
                    high_part(h, u, 0, 1, 0)
                if front and middle:
                    split_high(h, u, 0, 0, back)
                if front:
                    high_part(h, u, 0, 1, 1)
                if front and not middle:
                    split_high(h, u, 0, 0, back)
                if middle:
                    exponent(p - 1)
                if back and (front or middle):
                    out_to_sbuf(h - 1, u, 1, 0)
                if front and middle:
                    split_high(h, u, 0, 1, back)
                if front:
                    high_part(h, u, 1, 0, 0)
                if back and (front or middle):
                    out_to_sbuf(h - 1, u, 1, 1)
                if front:
                    high_part(h, u, 1, 0, 1)
                if front and middle:
                    split_high(h, u, 1, 0, back)
                if front and not middle:
                    split_high(h, u, 0, 1, back)
                if middle:
                    z_out(p - 1)
                if front:
                    high_part(h, u, 1, 1, 0)
                    gram_out(p, 0)
                    high_part(h, u, 1, 1, 1)
                if front and middle:
                    split_high(h, u, 1, 1, back)
                if front and not middle:
                    split_high(h, u, 1, 0, back)
                if middle:
                    pq_high(p - 1, 1 - u)
                if back and (front or middle):
                    normalise(h - 1, u, 0)
                if front:
                    gram_out(p, 1)
                if back and front:
                    normalise(h - 1, u, 1)
                if back and not front and not middle:
                    normalise_last(h - 1, u, 0, range(2))
                    normalise_last(h - 1, u, 1, range(1))

            steps(act, step)

        @block.vector
        def _(dve):
            dve.memset(attn[:, :, :], 0.0).then_inc(attn_zero, 1)
            dve.memset(t_hi[0][:, :, 2 * C:].bitcast(f32), 1.0).then_inc(ones_set, 1)
            dve.memset(t_hi[1][:, :, 2 * C:].bitcast(f32), 1.0).then_inc(ones_set, 1)
            dve.memset(gate[:, 1:2], 0.0).then_inc(o_out, 2)
            dve.memset(gate[:, 2:3], 0.0).then_inc(normed, 2)
            for n in range(4):
                dve.memset(gate[:, 3 + n:4 + n], 0.0).then_inc(stored[n], 16)
            dve.wait_ge(attn_zero, 1)

            def prepare():
                dve.wait_ge(consts_in, 16)
                dve.wait_ge(weights_in, 48)
                s0, s1 = float(C // H) ** -0.5, float(C) ** -0.5
                dve.tensor_scalar(w("qpT"), w("qpT"), s0, None, ALU.mult).then_inc(prepared, 1)
                dve.tensor_scalar(w("qrT"), w("qrT"), s0, None, ALU.mult).then_inc(prepared, 1)
                dve.tensor_scalar(w("qT"), w("qT"), s1, None, ALU.mult).then_inc(prepared, 1)
                dve.tensor_scalar(w("bq_rows"), w("bq_rows"), s1, None, ALU.mult).then_inc(prepared, 1)
                dve.tensor_scalar(nbq[:, :], col("bq"), s1 * N, None, ALU.mult).then_inc(prepared, 1)
                dve.wait_ge(prepared, 1)
                dve.tensor_copy(wk_hi[:, :, :], wt[:, 0:2, :]).then_inc(wkhi_ready, 1)
                dve.tensor_copy(mask6[:, 0:4, :], other_head.unsqueeze(1).broadcast_to([C, 4, W32]))
                dve.wait_ge(prepared, 5)
                for a in range(2):
                    last = dve.scalar_tensor_tensor(out=mask6[:, 4 + a, :], in0=bk32, scalar=nbq[:, :],
                                                    in1=other_head, op0=ALU.mult, op1=ALU.add)
                last.then_inc(prepared, 1)
                dve.wait_ge(wkhi_ready, 1)
                dve.tensor_tensor(wk_lo[:, :, :], wt[:, 0:2, :], wk_hi[:, :, :].bitcast(f32), ALU.subtract)\
                    .then_inc(prepared, 1)
                dve.wait_ge(prepared, 7)

            def y_transpose(h, u, b, i):
                slot = 2 * u + b
                t = 2 * (4 * h + slot) + i
                if i == 0:
                    dve.wait_ge(blocks_in[slot], 16 * QUADS * (h + 1))
                if not (isinstance(t, int) and t < 1):
                    dve.wait_ge(ylo_ready, t)
                blocks = y_blocks[slot][:, :, :].rearrange("p i (c m) -> p m i c", c=W32)
                dve.transpose(tpy[:, :, :].rearrange("p m (i c) -> p m i c", c=W32), blocks[:, HC * i:HC * (i + 1)])\
                    .then_inc(y_transposed, 1)

            def low_part(h, u, b, i, s):
                t = 2 * (4 * h + 2 * u + b) + i
                part = (slice(HC * i, HC * (i + 1)), slice(s * C, (s + 1) * C))
                dve.wait_ge((xhi_ready, yhi_ready)[s], t + 1)
                dve.tensor_tensor(t_lo[b][:, part[0], part[1]], (tpx, tpy)[s][:, :, :],
                                  t_hi[b][:, part[0], part[1]].bitcast(f32), ALU.subtract)\
                    .then_inc((xlo_ready, ylo_ready)[s], 1)

            def pq_low(p, parity):
                dve.wait_ge(pqhi_ready, p + 1)
                dve.tensor_tensor(pq_lo[parity][:, :, :, :].rearrange("p a s c -> p (a s c)"), mid1[:, :],
                                  pq_hi[parity][:, :, :, :].rearrange("p a s c -> p (a s c)").bitcast(f32),
                                  ALU.subtract).then_inc(pqlo_ready, 1)

            def half_stats(h, u, b, half):
                n = 4 * h + 2 * u + b
                dve.wait_ge(o_out, 2 * n + half + 3)
                dve.bn_stats(hstat[:, b, half, :], res[2 * u + b][:, half * HALF:(half + 1) * HALF])\
                    .then_inc(hstat_ready, 1)

            def half_stats_last(h, u, b, half):
                dve.wait_ge(o_done, 2 * (4 * h + 2 * u + b) + half + 1)
                dve.bn_stats(hstat[:, b, half, :], o_last[b][half][:, :]).then_inc(hstat_ready, 1)

            def half_moments(p, bs=BOTH):
                dve.wait_ge(hstat_ready, 4 * p + 2 * bs.stop)
                dve.memset(gate[:, 0:1], 0.0)
                for b in range(bs.start, bs.stop):
                    dve.bn_aggr(pstat[:, b, :], hstat[:, b, :, :]).then_inc(pstat_ready, 1)

            def partition_moments(p, u, bs=BOTH):
                count = p + 1 + bs.start
                dve.wait_ge(pstat_ready, 2 * p + bs.stop)
                dve.wait_ge(c_ready, p + 1)
                dve.tensor_tensor(mom[:, 0, bs], pstat[:, bs, 0], cshift[u][:, bs], ALU.add).then_inc(mean_ready, 1)
                dve.wait_ge(mean_ready, count)
                for b in range(bs.start, bs.stop):
                    mean = mom[:, 0, b:b + 1]
                    last = dve.scalar_tensor_tensor(out=mom[:, 1, b:b + 1], in0=mean, scalar=mean, in1=pstat[:, b, 1:2],
                                                    op0=ALU.mult, op1=ALU.add)
                last.then_inc(mom_ready, 1)

            def moments_out(p, bs=BOTH):
                dve.wait_ge(stat_done, p + 1 + bs.start)
                dve.tensor_tensor(gmom[:, :, bs], stat_mb[:, :, bs], zero_eps.rearrange("p (m b) -> p m b", b=2)[:, :, bs],
                                  ALU.add).then_inc(gmom_ready, 1)

            def neg_variance(p, u, bs=BOTH):
                dve.wait_ge(gmom_ready, p + 1 + bs.start)
                for b in range(bs.start, bs.stop):
                    mean = gmom[:, 0, b:b + 1]
                    last = dve.scalar_tensor_tensor(out=neg_var[:, b:b + 1], in0=mean, scalar=mean,
                                                    in1=gmom[:, 1, b:b + 1], op0=ALU.mult, op1=ALU.subtract)
                last.then_inc(neg_var_ready, 1)
                dve.tensor_tensor(cmu[:, bs], cshift[u][:, bs], gmom[:, 0, bs], ALU.subtract)

            def variance(p, bs=BOTH):
                dve.wait_ge(neg_var_ready, p + 1 + bs.start)
                dve.tensor_scalar(var[:, bs], neg_var[:, bs], -1.0, EPS, ALU.mult, ALU.max).then_inc(var_ready, 1)

            def norm_scale(p, bs=BOTH, last=False):
                count = p + 1 + bs.start
                dve.wait_ge(rstd_ready, count)
                if bs.start == 0:
                    dve.wait_ge(normed, 2 * p + (1 if last else 2))
                    if last:
                        dve.wait_ge(last_normed, 1)
                dve.tensor_scalar(nscale[:, bs], rstd[:, bs], col("gn_w"), None, ALU.mult).then_inc(nscale_ready, 1)
                dve.wait_ge(nscale_ready, count)
                for b in range(bs.start, bs.stop):
                    scaled = dve.scalar_tensor_tensor(out=nbias[:, b:b + 1], in0=cmu[:, b:b + 1],
                                                      scalar=nscale[:, b:b + 1], in1=col("gn_b"),
                                                      op0=ALU.mult, op1=ALU.add)
                scaled.then_inc(norm_ready, 1)

            def k_split(p):
                dve.wait_ge(gram_ready, 2 * p + 2)
                if not (isinstance(p, int) and p < 1):
                    dve.wait_ge(u12_done, p)
                dve.tensor_copy(k_hi[:, :, :], gram[:, :, 0:C]).then_inc(khi_ready, 1)
                dve.wait_ge(khi_ready, p + 1)
                dve.tensor_tensor(k_lo[:, :, :], gram[:, :, 0:C], k_hi[:, :, :].bitcast(f32), ALU.subtract)\
                    .then_inc(klo_ready, 1)

            def keys_times_sums(p):
                if not (isinstance(p, int) and p < 1):
                    dve.wait_ge(scores_done, p)
                dve.wait_ge(gram_ready, 2 * p + 2)
                for a in range(2):
                    last = dve.tensor_scalar(sk[:, a, :], w("kT"), gram[:, a, 2 * C:2 * C + 1], None, ALU.mult)
                last.then_inc(sk_ready, 1)

            def normalise_last(h, u, b, half):
                dve.wait_ge(norm_ready, 2 * h + u + 1 + b)
                dve.wait_ge(stored[2 * u + b], 16 * (h + 1))
                dve.tensor_scalar(res[2 * u + b][:, half * HALF:(half + 1) * HALF], o_last[b][half][:, :],
                                  nscale[:, b:b + 1], nbias[:, b:b + 1], ALU.mult, ALU.add).then_inc(last_normed, 1)

            def normalise(h, u, b):
                dve.wait_ge(norm_ready, 2 * h + u + 1)
                dve.tensor_scalar(res[2 * u + b][:, :], res[2 * u + b][:, :], nscale[:, b:b + 1], nbias[:, b:b + 1],
                                  ALU.mult, ALU.add).then_inc(last_normed, 1)

            def u3_out(p):
                dve.wait_ge(u3_done, p + 1)
                for a in range(2):
                    last = dve.scalar_tensor_tensor(out=u3[:, a, :], in0=w("bk_rows"),
                                                    scalar=gram[:, a, 2 * C:2 * C + 1],
                                                    in1=mid1[:, a * C:(a + 1) * C], op0=ALU.mult, op1=ALU.add)
                last.then_inc(u3_ready, 1)

            def shift_scores(p):
                dve.wait_ge(scores_done, p + 1)
                dve.tensor_tensor(sc_m[:, :, :], mid0[:, 0:6 * W32].rearrange("p (i c) -> p i c", c=W32),
                                  mask6[:, :, :], ALU.add).then_inc(masked, 1)
                dve.wait_ge(masked, p + 1)
                dve.tensor_reduce(smax[:, :], sc_m[:, :, :], AX.X, ALU.max).then_inc(max_ready, 1)
                dve.wait_ge(max_ready, p + 1)
                dve.tensor_tensor(sc_d[:, :, :], sc_m[:, :, :],
                                  smax[:, :].unsqueeze(2).broadcast_to([C, 6, W32]), ALU.subtract)\
                    .then_inc(shifted, 1)

            def softmax_out(p, quads=DVE_QUADS):
                dve.wait_ge(exp_ready, p + 1)
                dve.tensor_reduce(ssum[:, :], probs[:, :, :], AX.X, ALU.add).then_inc(sum_ready, 1)
                dve.tensor_tensor(abv_m[:, :, :], probs[:, 4:6, :], bv32.unsqueeze(1).broadcast_to([C, 2, W32]),
                                  ALU.mult).then_inc(abv_step, 1)
                dve.wait_ge(sum_ready, p + 1)
                dve.reciprocal(sinv[:, :], ssum[:, :]).then_inc(inv_ready, 1)
                dve.wait_ge(abv_step, 2 * p + 1)
                dve.tensor_reduce(abv_s[:, :], abv_m[:, :, :], AX.X, ALU.add).then_inc(abv_step, 1)
                dve.wait_ge(inv_ready, p + 1)
                for j in range(quads):
                    q = slice(W32 * j, W32 * (j + 1))
                    last = dve.tensor_tensor(attn[q, :, q], probs[q, :, :],
                                             sinv[q, :].unsqueeze(2).broadcast_to([W32, 6, W32]), ALU.mult)
                last.then_inc(attn_dve_ready, 1)
                dve.wait_ge(abv_step, 2 * p + 2)
                dve.tensor_tensor(abv[:, :], abv_s[:, :], sinv[:, 4:6], ALU.mult).then_inc(abv_ready, 1)

            def n12_out(p):
                dve.wait_ge(m12_done, p + 1)
                dve.tensor_tensor(nmat[:, 0:2, :, :].rearrange("p i a c -> p (i a) c"),
                                  mid1[:, :].rearrange("p (i c) -> p i c", c=C),
                                  ident.unsqueeze(1).broadcast_to([C, 4, C]), ALU.add)

            def n3_out(p):
                dve.wait_ge(m3_done, p + 1)
                dve.wait_ge(wo_abv_done, p + 1)
                dve.tensor_tensor(nmat[:, 2, :, :], mid0[:, 0:2 * C].rearrange("p (i c) -> p i c", c=C),
                                  ident.unsqueeze(1).broadcast_to([C, 2, C]), ALU.add).then_inc(n_ready, 1)

            def c_out(p, parity):
                dve.wait_ge(wo_abv_done, p + 1)
                dve.tensor_scalar(cshift[parity][:, :], mid0[:, 2 * C:2 * C + 2], col("bo"), None, ALU.add)\
                    .then_inc(c_ready, 1)

            def step(h, u, front, middle, back):
                p = 2 * h + u
                if front:
                    y_transpose(h, u, 0, 0)
                if middle:
                    k_split(p - 1)
                    keys_times_sums(p - 1)
                if front:
                    low_part(h, u, 0, 0, 0)
                    low_part(h, u, 0, 0, 1)
                if middle:
                    u3_out(p - 1)
                if back and (front or middle):
                    half_stats(h - 1, u, 0, 0)
                if front:
                    y_transpose(h, u, 0, 1)
                if back and front:
                    half_stats(h - 1, u, 0, 1)
                if front:
                    low_part(h, u, 0, 1, 0)
                if middle:
                    shift_scores(p - 1)
                if middle and not front:
                    half_stats(h - 1, u, 0, 1)
                if front:
                    low_part(h, u, 0, 1, 1)
                if front and middle:
                    softmax_out(p - 1)
                if middle and not front:
                    softmax_out(p - 1, LAST_DVE_QUADS)
                if front:
                    y_transpose(h, u, 1, 0)
                if back and (front or middle):
                    half_stats(h - 1, u, 1, 0)
                if front:
                    low_part(h, u, 1, 0, 0)
                if back and (front or middle):
                    half_stats(h - 1, u, 1, 1)
                    half_moments(p - 2)
                    partition_moments(p - 2, u)
                if front:
                    low_part(h, u, 1, 0, 1)
                    y_transpose(h, u, 1, 1)
                if back and (front or middle):
                    moments_out(p - 2)
                    neg_variance(p - 2, u)
                if middle:
                    n12_out(p - 1)
                if back and (front or middle):
                    variance(p - 2)
                if middle:
                    n3_out(p - 1)
                if front:
                    low_part(h, u, 1, 1, 0)
                    low_part(h, u, 1, 1, 1)
                if front and not middle:
                    prepare()
                if middle:
                    c_out(p - 1, 1 - u)
                if back and (front or middle):
                    norm_scale(p - 2)
                if middle:
                    pq_low(p - 1, 1 - u)
                if middle and not front:
                    normalise(h - 1, u, 1)
                if back and not front and not middle:
                    half_stats_last(h - 1, u, 0, 0)
                    half_stats_last(h - 1, u, 0, 1)
                    half_moments(p - 2, slice(0, 1))
                    partition_moments(p - 2, u, slice(0, 1))
                    half_stats_last(h - 1, u, 1, 0)
                    moments_out(p - 2, slice(0, 1))
                    neg_variance(p - 2, u, slice(0, 1))
                    variance(p - 2, slice(0, 1))
                    half_stats_last(h - 1, u, 1, 1)
                    half_moments(p - 2, slice(1, 2))
                    partition_moments(p - 2, u, slice(1, 2))
                    norm_scale(p - 2, slice(0, 1), True)
                    moments_out(p - 2, slice(1, 2))
                    neg_variance(p - 2, u, slice(1, 2))
                    variance(p - 2, slice(1, 2))
                    norm_scale(p - 2, slice(1, 2), True)
                    normalise_last(h - 1, u, 1, 1)

            steps(dve, step)

        @block.gpsimd
        def _(pool):
            pool.wait_ge(consts_in, 16)

            def softmax_out(p, split, first=DVE_QUADS):
                pool.wait_ge(split_lo, split)
                if isinstance(p, int) and p == 0:
                    pool.wait_ge(attn_zero, 1)
                else:
                    pool.wait_ge(z_done, p)
                pool.wait_ge(inv_ready, p + 1)
                for j in range(first, QUADS):
                    q = slice(W32 * j, W32 * (j + 1))
                    last = pool.tensor_tensor(attn[q, :, q], probs[q, :, :],
                                              sinv[q, :].unsqueeze(2).broadcast_to([W32, 6, W32]), ALU.mult)
                last.then_inc(attn_pool_ready, 1)
                pool.wait_ge(attn_pool_ready, p + 1)

            def split_low(h, u, b, s):
                slot = 2 * u + b
                pool.wait_ge(split_hi, 2 * (4 * h + slot) + s + 1)
                for c in range(PIECES):
                    cols = slice(c * N // PIECES, (c + 1) * N // PIECES)
                    piece = pool.tensor_tensor(xy_lo[slot][:, s, cols], raw[slot][:, s, cols],
                                               xy_hi[slot][:, s, cols].bitcast(f32), ALU.subtract)
                piece.then_inc(split_lo, 1)

            def deviation(p, bs=BOTH):
                pool.wait_ge(var_ready, p + 1 + bs.start)
                pool.tensor_tensor(rstd[:, bs], var[:, bs], neg_half[:, bs], ALU.pow).then_inc(rstd_ready, 1)

            def step(h, u, front, middle, back):
                p = 2 * h + u
                if middle:
                    if front:
                        softmax_out(p - 1, 2 * (4 * h + 2 * u))
                    else:
                        softmax_out(p - 1, 2 * B, LAST_DVE_QUADS)
                if front:
                    split_low(h, u, 0, 0)
                    split_low(h, u, 0, 1)
                if back and (front or middle):
                    deviation(p - 2)
                elif back:
                    for b in range(2):
                        deviation(p - 2, slice(b, b + 1))
                if front:
                    split_low(h, u, 1, 0)
                    split_low(h, u, 1, 1)

            steps(pool, step)


def kernel(**inputs):
    import numpy as np
    import concourse.bacc as _bacc
    from concourse import mybir as _mybir
    from concourse.bass_utils import run_bass_kernel_spmd as _run

    a = {k: np.asarray(v) for k, v in inputs.items()}
    l0 = lambda k: a["L0_xattn_" + k]
    l1 = lambda k: a["L1_xattn_" + k]
    rows = lambda v: np.broadcast_to(v[None, :], (C, C))
    mats = {"kpT": l0("wk_point").T, "qpT": l0("wq_point").T, "kT": l1("Wk").T, "qrT": l0("wq_rgb").T,
            "krT": l0("wk_rgb").T, "qT": l1("Wq").T, "vp": l0("wv_point"), "vr": l0("wv_rgb"),
            "oT": l1("Wo").T, "ppT": l0("proj_p2r").T, "prT": l0("proj_r2p").T, "v": l1("Wv"),
            "bk_rows": rows(l1("bk")), "bq_rows": rows(l1("bq"))}
    weights = np.ascontiguousarray(np.stack([mats[k] for k in WNAMES], axis=1))
    vectors = np.ascontiguousarray(np.stack([l1(k) for k in VNAMES], axis=1))
    quad_rows = np.ascontiguousarray(np.stack(
        [np.repeat(l1(k).reshape(QUADS, W32), W32, axis=0) for k in ("bk", "bv")], axis=1))

    ch = np.arange(C)
    w32 = np.arange(W32)
    consts = np.concatenate([
        np.eye(C), np.full((C, C), 1.0 / C),
        np.where((ch[:, None] % W32) // (C // H) == w32[None, :] // (C // H), 0.0, NEG),
        np.zeros((C, 2)), np.full((C, 2), EPS), np.full((C, 2), -0.5)], axis=1).astype(np.float32)

    nc = _bacc.Bacc("TRN2", target_bir_lowering=False, num_devices=1)
    arrays = {"x": np.ascontiguousarray(a["x"]), "ctx": np.ascontiguousarray(a["ctx_4096"]), "weights": weights,
              "vectors": vectors, "quad_rows": quad_rows, "consts": consts}
    args = [nc.dram_tensor(f"in_{k}", v.shape, _mybir.dt.from_np(v.dtype), kind="ExternalInput").ap()
            for k, v in arrays.items()]
    out = nc.dram_tensor("out", (B, C, N), _mybir.dt.float32, kind="ExternalOutput").ap()
    cross_attention_pair_kernel(nc, *args, out)
    r = _run(nc, [{f"in_{k}": v for k, v in arrays.items()}], core_ids=[0])
    return r.results[0]["out"]
```
